# Optimizing a Trainium2 kernel written in Bass

```python
import numpy as np
import jax
import jax.numpy as jnp

def _softmax(x, axis=-1):
    return jax.nn.softmax(x, axis=axis)

def _gelu(x):
    return jax.nn.gelu(x, approximate=True)

def _silu(x):
    return jax.nn.silu(x)

def _sigmoid(x):
    return jax.nn.sigmoid(x)

def _layernorm(x, axis=-1, eps=1e-05):
    m = jnp.mean(x, axis=axis, keepdims=True)
    v = jnp.var(x, axis=axis, keepdims=True)
    return (x - m) / jnp.sqrt(v + eps)

def _scatter_add(tgt, idx, src, axis=0):
    return tgt.at[idx].add(src)

def _segment_sum(src, seg, n):
    return jax.ops.segment_sum(src, seg, n)
kernel_name = 'mk_seq_postln_d1_jaxref_r8_b098d6'

def setup_inputs(seed: int=0):
    np.random.seed(seed)
    _w = jnp.asarray

    def _L0_attn_setup():
        import jax, jax.numpy as jnp
        import numpy as np
        import math
        DIM = 256
        N_HEADS = 16
        Q_LORA = 64
        KV_LORA = 64
        NOPE = 128
        ROPE = 64
        QK_HD = NOPE + ROPE
        V_HD = 128
        THETA = 1000000.0

        def _linear_params(key, fan_in, fan_out):
            kw, kb = jax.random.split(key)
            w = jax.random.normal(kw, (fan_in, fan_out), jnp.float32) * 0.02
            b = jax.random.normal(kb, (fan_out,), jnp.float32) * 0.02
            return (w, b)

        def _rope_cos_sin(seq_len):
            inv_freq = 1.0 / THETA ** (jnp.arange(0, ROPE, 2, dtype=jnp.float32) / ROPE)
            t = jnp.arange(seq_len, dtype=jnp.float32)
            freqs = jnp.outer(t, inv_freq)
            return (jnp.cos(freqs), jnp.sin(freqs))

        def _apply_rope(x, cos, sin):
            xr = x[..., 0::2]
            xi = x[..., 1::2]
            c = cos[None, :, None, :]
            s = sin[None, :, None, :]
            out_r = xr * c - xi * s
            out_i = xr * s + xi * c
            return jnp.stack([out_r, out_i], axis=-1).reshape(x.shape)
        key = jax.random.key(seed)
        ks = jax.random.split(key, 6)
        x = jax.random.normal(ks[0], (2, 256, DIM), jnp.float32)
        wq_a_w, wq_a_b = _linear_params(ks[1], DIM, Q_LORA)
        wq_b_w, wq_b_b = _linear_params(ks[2], Q_LORA, N_HEADS * QK_HD)
        wkv_a_w, wkv_a_b = _linear_params(ks[3], DIM, KV_LORA + ROPE)
        wkv_b_w, wkv_b_b = _linear_params(ks[4], KV_LORA, N_HEADS * (NOPE + V_HD))
        wo_w, wo_b = _linear_params(ks[5], N_HEADS * V_HD, DIM)
        return {'x': x, 'wq_a_w': wq_a_w, 'wq_a_b': wq_a_b, 'wq_b_w': wq_b_w, 'wq_b_b': wq_b_b, 'wkv_a_w': wkv_a_w, 'wkv_a_b': wkv_a_b, 'wkv_b_w': wkv_b_w, 'wkv_b_b': wkv_b_b, 'wo_w': wo_w, 'wo_b': wo_b}
    _L0_attn_in = _L0_attn_setup()

    def _L0_ffn_setup():
        import jax, jax.numpy as jnp
        import numpy as np
        B, S, D = (4, 256, 256)
        E = 8
        N_SHARE = 2
        N_ROUTED = E - N_SHARE
        H = 1024 // E
        key = jax.random.key(seed)
        ks = jax.random.split(key, 12)
        s = 0.02
        return {'x': jax.random.normal(ks[0], (B, S, D), jnp.float32), 'Wg': jax.random.normal(ks[1], (D, E), jnp.float32) * s, 'bg': jnp.zeros((E,), jnp.float32), 'Wgate': jax.random.normal(ks[2], (N_ROUTED, D, H), jnp.float32) * s, 'bgate': jnp.zeros((N_ROUTED, H), jnp.float32), 'Wup': jax.random.normal(ks[3], (N_ROUTED, D, H), jnp.float32) * s, 'bup': jnp.zeros((N_ROUTED, H), jnp.float32), 'Wdown': jax.random.normal(ks[4], (N_ROUTED, H, D), jnp.float32) * s, 'bdown': jnp.zeros((N_ROUTED, D), jnp.float32), 'Ws_up': jax.random.normal(ks[5], (D, N_SHARE * H), jnp.float32) * s, 'bs_up': jnp.zeros((N_SHARE * H,), jnp.float32), 'Ws_down': jax.random.normal(ks[6], (N_SHARE * H, D), jnp.float32) * s, 'bs_down': jnp.zeros((D,), jnp.float32)}
    _L0_ffn_in = _L0_ffn_setup()
    _d = {'L0_attn_x': _L0_attn_in['x'], 'L0_attn_wq_a_w': _L0_attn_in['wq_a_w'], 'L0_attn_wq_a_b': _L0_attn_in['wq_a_b'], 'L0_attn_wq_b_w': _L0_attn_in['wq_b_w'], 'L0_attn_wq_b_b': _L0_attn_in['wq_b_b'], 'L0_attn_wkv_a_w': _L0_attn_in['wkv_a_w'], 'L0_attn_wkv_a_b': _L0_attn_in['wkv_a_b'], 'L0_attn_wkv_b_w': _L0_attn_in['wkv_b_w'], 'L0_attn_wkv_b_b': _L0_attn_in['wkv_b_b'], 'L0_attn_wo_w': _L0_attn_in['wo_w'], 'L0_attn_wo_b': _L0_attn_in['wo_b'], 'L0_ffn_Wg': _L0_ffn_in['Wg'], 'L0_ffn_bg': _L0_ffn_in['bg'], 'L0_ffn_Wgate': _L0_ffn_in['Wgate'], 'L0_ffn_bgate': _L0_ffn_in['bgate'], 'L0_ffn_Wup': _L0_ffn_in['Wup'], 'L0_ffn_bup': _L0_ffn_in['bup'], 'L0_ffn_Wdown': _L0_ffn_in['Wdown'], 'L0_ffn_bdown': _L0_ffn_in['bdown'], 'L0_ffn_Ws_up': _L0_ffn_in['Ws_up'], 'L0_ffn_bs_up': _L0_ffn_in['bs_up'], 'L0_ffn_Ws_down': _L0_ffn_in['Ws_down'], 'L0_ffn_bs_down': _L0_ffn_in['bs_down']}
    _x0 = _d['L0_attn_x']
    _d['L0_attn_x'] = jax.random.normal(jax.random.fold_in(jax.random.key(seed), 1), (8, 512, 256), dtype=_x0.dtype)
    del _x0
    return _d

def reference(L0_attn_x, L0_attn_wq_a_w, L0_attn_wq_a_b, L0_attn_wq_b_w, L0_attn_wq_b_b, L0_attn_wkv_a_w, L0_attn_wkv_a_b, L0_attn_wkv_b_w, L0_attn_wkv_b_b, L0_attn_wo_w, L0_attn_wo_b, L0_ffn_Wg, L0_ffn_bg, L0_ffn_Wgate, L0_ffn_bgate, L0_ffn_Wup, L0_ffn_bup, L0_ffn_Wdown, L0_ffn_bdown, L0_ffn_Ws_up, L0_ffn_bs_up, L0_ffn_Ws_down, L0_ffn_bs_down):

    def _L0_attn_ref(x, wq_a_w, wq_a_b, wq_b_w, wq_b_b, wkv_a_w, wkv_a_b, wkv_b_w, wkv_b_b, wo_w, wo_b):
        import jax, jax.numpy as jnp
        import numpy as np
        import math
        DIM = 256
        N_HEADS = 16
        Q_LORA = 64
        KV_LORA = 64
        NOPE = 128
        ROPE = 64
        QK_HD = NOPE + ROPE
        V_HD = 128
        THETA = 1000000.0

        def _linear_params(key, fan_in, fan_out):
            kw, kb = jax.random.split(key)
            w = jax.random.normal(kw, (fan_in, fan_out), jnp.float32) * 0.02
            b = jax.random.normal(kb, (fan_out,), jnp.float32) * 0.02
            return (w, b)

        def _rope_cos_sin(seq_len):
            inv_freq = 1.0 / THETA ** (jnp.arange(0, ROPE, 2, dtype=jnp.float32) / ROPE)
            t = jnp.arange(seq_len, dtype=jnp.float32)
            freqs = jnp.outer(t, inv_freq)
            return (jnp.cos(freqs), jnp.sin(freqs))

        def _apply_rope(x, cos, sin):
            xr = x[..., 0::2]
            xi = x[..., 1::2]
            c = cos[None, :, None, :]
            s = sin[None, :, None, :]
            out_r = xr * c - xi * s
            out_i = xr * s + xi * c
            return jnp.stack([out_r, out_i], axis=-1).reshape(x.shape)
        bs, seq_len, _ = x.shape
        q = (x @ wq_a_w + wq_a_b) @ wq_b_w + wq_b_b
        q = q.reshape(bs, seq_len, N_HEADS, QK_HD)
        q_nope, q_pe = (q[..., :NOPE], q[..., NOPE:])
        ckv = x @ wkv_a_w + wkv_a_b
        compressed_kv, k_pe = (ckv[..., :KV_LORA], ckv[..., KV_LORA:])
        k_pe = k_pe.reshape(bs, seq_len, 1, ROPE)
        kv = (compressed_kv @ wkv_b_w + wkv_b_b).reshape(bs, seq_len, N_HEADS, NOPE + V_HD)
        kv_nope, v = (kv[..., :NOPE], kv[..., NOPE:])
        cos, sin = _rope_cos_sin(seq_len)
        q_pe = _apply_rope(q_pe, cos, sin)
        k_pe = _apply_rope(k_pe, cos, sin)
        k_pe = jnp.broadcast_to(k_pe, (bs, seq_len, N_HEADS, ROPE))
        qf = jnp.concatenate([q_nope, q_pe], axis=-1)
        kf = jnp.concatenate([kv_nope, k_pe], axis=-1)
        scores = jnp.einsum('bqhd,bkhd->bhqk', qf, kf) / math.sqrt(V_HD)
        probs = jax.nn.softmax(scores.astype(jnp.float32), axis=-1).astype(qf.dtype)
        out = jnp.einsum('bhqk,bkhd->bqhd', probs, v)
        out = out.reshape(bs, seq_len, N_HEADS * V_HD)
        return out @ wo_w + wo_b

    def _L0_ffn_ref(x, Wg, bg, Wgate, bgate, Wup, bup, Wdown, bdown, Ws_up, bs_up, Ws_down, bs_down):
        import jax, jax.numpy as jnp
        import numpy as np
        B, S, D = (4, 256, 256)
        E = 8
        N_SHARE = 2
        N_ROUTED = E - N_SHARE
        H = 1024 // E
        b, s, d = x.shape
        T = b * s
        n = Wgate.shape[0]
        xf = x.reshape(T, d)
        gate = xf @ Wg + bg
        vals, ids = jax.lax.top_k(gate, n)
        rows = jnp.arange(T)[:, None]
        masked = jnp.full_like(gate, -jnp.inf).at[rows, ids].set(vals)
        probs = jax.nn.softmax(masked, axis=-1)
        routed_mask = (ids[:, :, None] == jnp.arange(n)).any(axis=1)
        w = probs[:, :n] * routed_mask
        g = jnp.einsum('td,ndh->tnh', xf, Wgate) + bgate
        u = jnp.einsum('td,ndh->tnh', xf, Wup) + bup
        h = jax.nn.silu(g) * u
        eo = jnp.einsum('tnh,nhd->tnd', h, Wdown) + bdown
        routed_out = jnp.einsum('tnd,tn->td', eo, w)
        share = jax.nn.silu(xf @ Ws_up + bs_up) @ Ws_down + bs_down
        return (routed_out + share).reshape(b, s, d)
    x = L0_attn_x
    x = _layernorm(x + _L0_attn_ref(x, L0_attn_wq_a_w, L0_attn_wq_a_b, L0_attn_wq_b_w, L0_attn_wq_b_b, L0_attn_wkv_a_w, L0_attn_wkv_a_b, L0_attn_wkv_b_w, L0_attn_wkv_b_b, L0_attn_wo_w, L0_attn_wo_b), axis=-1)
    x = _layernorm(x + _L0_ffn_ref(x, L0_ffn_Wg, L0_ffn_bg, L0_ffn_Wgate, L0_ffn_bgate, L0_ffn_Wup, L0_ffn_bup, L0_ffn_Wdown, L0_ffn_bdown, L0_ffn_Ws_up, L0_ffn_bs_up, L0_ffn_Ws_down, L0_ffn_bs_down), axis=-1)
    return x

_drawn_inputs = setup_inputs


def setup_inputs(seed=0):
    import zlib

    import numpy as np

    out = dict(_drawn_inputs(seed))
    spreads = {'L0_ffn_bg': (0.0, 0.8),
     'L0_ffn_bgate': (0.0, 0.8),
     'L0_ffn_bup': (0.0, 0.8),
     'L0_ffn_bdown': (0.0, 0.67),
     'L0_ffn_bs_up': (0.0, 1.234),
     'L0_ffn_bs_down': (0.0, 0.1)}
    factors = {'L0_attn_wq_a_w': 8.0,
     'L0_attn_wq_a_b': 8.0,
     'L0_attn_wq_b_w': 8.0,
     'L0_attn_wq_b_b': 8.0,
     'L0_attn_wkv_a_w': 8.0,
     'L0_attn_wkv_a_b': 8.0,
     'L0_attn_wkv_b_w': 8.0,
     'L0_attn_wkv_b_b': 3.176,
     'L0_attn_wo_w': 3.134,
     'L0_attn_wo_b': 2.934,
     'L0_ffn_Wg': 2.849,
     'L0_ffn_Wgate': 8.0,
     'L0_ffn_Wup': 8.0,
     'L0_ffn_Wdown': 8.0,
     'L0_ffn_Ws_up': 3.069}
    for name, (base, spread) in spreads.items():
        noise = np.random.default_rng([zlib.crc32(name.encode()), seed]).standard_normal(out[name].shape)
        drawn = base * np.exp(spread * noise) if base else spread * noise
        out[name] = jnp.asarray(drawn.astype(out[name].dtype))
    for name, factor in factors.items():
        out[name] = (out[name] * factor).astype(out[name].dtype)
    return out
```

```python
from contextlib import ExitStack

import numpy as np
import concourse.bass as bass
from concourse import mybir

F32 = mybir.dt.float32
F32R = mybir.dt.float32r
ALU = mybir.AluOpType
ACT = mybir.ActivationFunctionType
AX = mybir.AxisListType

P = 128
BATCH, SEQ, DIM = 8, 512, 256
HEADS, NOPE, ROPE, VHD = 16, 128, 64, 128
RANK = 64
PAIRS = HEADS // 2
DC = DIM // P
TT = SEQ // P
EXPERTS, ROUTED, HID = 8, 6, 128
SHARED = 2
UNITS = ROUTED + SHARED
EPS = 1e-5
THETA = 1000000.0
SCALE = 1.0 / float(np.sqrt(VHD))
TILES = 2 * TT
ROUTE_STEPS, ROUTE_EXP = 13, 3


def program(nc, t, out):
    ctx = ExitStack()
    with ctx:
        def sb(name, shape, dt=F32):
            return ctx.enter_context(nc.sbuf_tensor(name, shape, dt))

        def sem(name):
            return ctx.enter_context(nc.semaphore(name))

        def sems(name, n):
            return [sem(f"{name}{i}") for i in range(n)]

        x1_dram = nc.dram_tensor("x1_scratch", (BATCH, P, TT * DIM), F32, kind="Internal").ap()

        bank = [ctx.enter_context(nc.psum_tensor(f"bank{i}", [P, 512], F32)) for i in range(8)]
        s_bank, pt_bank, q_bank, u_bank = bank[0:2], bank[2:4], bank[4:7], bank[7]

        arena = sb("arena", [P, 13312])

        def view(at, n):
            return arena[:, at:at + n]
        wq_raw = view(0, 3072).rearrange("p (a c m) -> p a c m", a=PAIRS, c=3)
        wqn = view(3072, 2048).rearrange("p (h i) -> p h i", h=HEADS)
        wkn = view(5120, 1024).rearrange("p (h j) -> p h j", h=HEADS)
        wv = view(6144, 1024).rearrange("p (h j) -> p h j", h=HEADS)
        wo = view(7168, 4096).rearrange("p (h n) -> p h n", h=HEADS)
        bv_wide = view(11264, 2048).rearrange("p (h m) -> p h m", h=HEADS)
        probs = view(0, 8192).rearrange("p (m j k) -> p m j k", m=2, j=TILES)
        probs_t = view(8192, 4096).rearrange("p (k q) -> p k q", k=TILES)

        ident = sb("ident", [P, P])
        rope = sb("rope", [P, 6, SEQ])
        w_a = sb("w_a", [P, DC, 4, P])
        b_a = sb("b_a", [P, 4])
        b_kv = sb("b_kv", [P, RANK])
        b_qn = sb("b_qn", [P, HEADS])
        b_v = sb("b_v", [P, HEADS])
        b_o = sb("b_o", [P, DIM])
        b_q = sb("b_q", [P, PAIRS, 4])
        ones = sb("ones", [P, P])
        wq_split = sb("wq_split", [P, PAIRS, 2, 3 * P], F32R)
        wq_stage = sb("wq_stage", [P, 2, 2, 3 * P], F32R)
        g_hi = sb("g_hi", [P, PAIRS, DIM], F32R)
        g_lo = sb("g_lo", [P, PAIRS, DIM], F32R)
        x_t = sb("x_t", [P, DC, SEQ])
        x_tok = sb("x_tok", [P, TT, DIM])
        x_b = sb("x_b", [P, TT, DIM])
        z = sb("z", [P, TT, DIM])
        x1 = sb("x1", [P, TT, DIM])
        stats = sb("stats", [P, TT, 6])
        mv = sb("mv", [P, TT, 2])
        var_e = sb("var_e", [P, TT])
        rstd = sb("rstd", [P, TT])
        minus_half = sb("minus_half", [P, TT])
        cq_raw = sb("cq_raw", [P, SEQ])
        cq = sb("cq", [P, SEQ], F32R)
        k_hi = sb("k_hi", [P, 2, SEQ], F32R)
        k_lo = sb("k_lo", [P, 2, SEQ], F32R)
        v_lat = sb("v_lat", [P, TT, RANK])
        roped = sb("roped", [P, 2, SEQ])
        rot = sb("rot", [P, SEQ])
        q_hi = sb("q_hi", [P, 2, 2, SEQ], F32R)
        q_lo = sb("q_lo", [P, 2, 2, SEQ], F32R)
        neg_max = sb("neg_max", [P, 2, TILES])
        sums = sb("sums", [P, 2, TILES])
        inv = sb("inv", [P, 2, TILES])
        u_hi = sb("u_hi", [P, PAIRS, SEQ], F32R)
        u_lo = sb("u_lo", [P, PAIRS, SEQ], F32R)

        flat = "p a c m -> p (a c m)"
        n_in, n_sh = DC * 2 * ROUTED * HID, DC * SHARED * HID
        w_in_v = wq_split[:].rearrange("p a c m -> p (a c m)").rearrange(
            "p (s d u m) -> p s d u m", s=2, d=DC, u=2 * ROUTED)
        w_sh_v = wq_stage[:].rearrange("p a c m -> p (a c m)")[:, 0:2 * DC * SHARED * HID].rearrange(
            "p (s d u m) -> p s d u m", s=2, d=DC, u=SHARED)
        w_out_hi, w_out_lo = g_hi, g_lo
        h_hi, h_lo = u_hi, u_lo
        y_raw, y_hi, y_lo = roped, k_hi, k_lo
        y_tok, y_res = x_tok, x_b
        sel = q_hi[0:EXPERTS].rearrange("p a c m -> p (a c m)")[:, 0:ROUTED * P].rearrange(
            "p (u m) -> p u m", u=ROUTED)
        w_t_split = q_lo[0:EXPERTS, 0]
        raw_in = view(0, DC * 2 * ROUTED * HID)
        raw_sh = view(3072, DC * SHARED * HID)
        raw_out = view(3584, UNITS * DIM).rearrange("p (u n) -> p u n", u=UNITS)
        half_pre = view(5632, 2 * SEQ).rearrange("p (m q) -> p m q", m=2)
        tanh_pre = view(6656, 2 * SEQ).rearrange("p (m q) -> p m q", m=2)
        hidden = view(7680, 2 * SEQ).rearrange("p (m q) -> p m q", m=2)
        w_g = sb("w_g", [P, DC, EXPERTS])
        b_g = sb("b_g", [P, EXPERTS])
        b_pre = sb("b_pre", [P, UNITS])
        b_up = sb("b_up", [P, UNITS])
        b_down = sb("b_down", [EXPERTS, DIM])
        sel_raw = view(8704, ROUTED * P)[0:EXPERTS].rearrange("p (u m) -> p u m", u=ROUTED)
        before = sb("before", [P, EXPERTS * EXPERTS])
        gate = sb("gate", [P, TT, EXPERTS])
        above = view(9472, 256).rearrange("p (t e f) -> p t e f", t=TT, e=EXPERTS)
        ties = view(9728, 256).rearrange("p (t e f) -> p t e f", t=TT, e=EXPERTS)
        rank = sb("rank", [P, TT, EXPERTS])
        chosen = sb("chosen", [P, TT, EXPERTS])
        top = sb("top", [P, TT])
        shifted = sb("shifted", [P, TT, EXPERTS])
        odds = sb("odds", [P, TT, EXPERTS])
        picked = sb("picked", [P, TT, EXPERTS])
        total = sb("total", [P, TT])
        inv_total = sb("inv_total", [P, TT])
        w_tok = sb("w_tok", [P, TT, EXPERTS])
        w_t = view(9984, SEQ)[0:EXPERTS]

        w_loaded = sem("w_loaded")
        consts_set = sem("consts_set")
        bv_wide_set = sem("bv_wide_set")
        m_made = sem("m_made")
        g_made = sem("g_made")
        wq_full = sem("wq_full")
        wq_hi_set = sem("wq_hi_set")
        wq_lo_set = sem("wq_lo_set")
        g_hi_set = sem("g_hi_set")
        attn_w_set = sem("attn_w_set")
        xt_loaded, x_loaded = sem("xt_loaded"), sem("x_loaded")
        proj = sems("proj", 5)
        cq_raw_set, cq_hi_set, cq_set = sem("cq_raw_set"), sem("cq_hi_set"), sem("cq_set")
        k_part, k_full, k_hi_set, k_lo_set = sem("k_part"), sem("k_full"), sem("k_hi_set"), sem("k_lo_set")
        v_set = sem("v_set")
        xb_set = sem("xb_set")
        oproj = sems("oproj", TT)
        z_set = sems("z_set", TT)
        stats_set, mv_set, var_set, rstd_set, x1_set = (sem("stats_set"), sem("mv_set"), sem("var_set"),
                                                        sem("rstd_set"), sem("x1_set"))
        x1_stored = sem("x1_stored")
        staged = sems("staged", 2)
        qproj = sems("qproj", 3)
        q_cos = sem("q_cos")
        q_added0, q_added, q_hi_set, q_lo_set = sem("q_added0"), sem("q_added"), sem("q_hi_set"), sem("q_lo_set")
        scores = sems("scores", TILES)
        rowmax = sems("rowmax", TILES)
        exp_done = sems("exp_done", TILES)
        inv_set = sems("inv_set", TILES)
        probs_set = sems("probs_set", 2)
        turned = sems("turned", TILES)
        pt_set = sems("pt_set", TILES)
        pv = sems("pv", TT)
        u_hi_set = sem("u_hi_set")
        u_set = sem("u_set")

        fw_loaded, fw_const, fw_hi_set, fw_lo_set, b_half_set = (
            sem("fw_loaded"), sem("fw_const"), sem("fw_hi_set"), sem("fw_lo_set"), sem("b_half_set"))
        y_loaded, y_turned, y_raw_set, y_hi_set, y_lo_set, y_res_loaded = (
            sem("y_loaded"), sem("y_turned"), sem("y_raw_set"), sem("y_hi_set"), sem("y_lo_set"), sem("y_res_loaded"))
        routed = sem("routed")
        route_step = sem("route_step")
        odds_set, w_turned, w_t_set, w_hi_set, w_lo_set = (
            sem("odds_set"), sem("w_turned"), sem("w_t_set"), sem("w_hi_set"), sem("w_lo_set"))
        pre = sems("pre", 2)
        half_set = sems("half_set", 2)
        tanh_set = sems("tanh_set", 2)
        silu_set = sems("silu_set", 2)
        gated = sems("gated", 2)
        widened = sems("widened", 2)
        h_set = sems("h_set", 2)
        h_hi_set = sems("h_hi_set", 2)
        h_lo_set = sems("h_lo_set", 2)
        down = sems("down", TT)
        z2_set = sems("z2_set", TT)
        stats2_set, mv2_set, var2_set, rstd2_set, out_set = (
            sem("stats2_set"), sem("mv2_set"), sem("var2_set"), sem("rstd2_set"), sem("out_set"))
        stored = sem("stored")

        block = ctx.enter_context(nc.Block())

        class Item:
            def __init__(self, eng, b, pair, buf):
                self.pair, self.buf = pair, buf
                self.n1 = eng.snap(b * PAIRS + pair + 1)
                self.n2 = eng.snap(b * PAIRS + pair + 2)

        def walk(eng, b, step):
            def item(i, buf):
                return Item(eng, b, i, buf)
            first = item(0, 0)
            step(None, None, first)
            second = item(1, 1)
            step(None, first, second)
            with eng.Fori(0, PAIRS // 2 - 1) as i:
                a0, a1, a2, a3 = item(2 * i, 0), item(2 * i + 1, 1), item(2 * i + 2, 0), item(2 * i + 3, 1)
                step(a0, a1, a2)
                step(a1, a2, a3)
            last = item(PAIRS - 1, 1)
            step(item(PAIRS - 2, 0), last, None)
            step(last, None, None)

        @block.sync
        def _(sp):
            for dst, src in ((wqn, t["wqn"]), (wkn, t["wkn"]), (wv, t["wv"]), (wo, t["wo"]),
                             (wq_raw, t["wq_raw"]), (b_qn[:], t["b_qn"]), (b_v[:], t["b_v"]),
                             (b_q[:], t["b_q"]), (ident[:], t["ident"]), (b_a[:], t["b_a"]),
                             (w_a[:], t["w_a"]), (rope[:], t["rope"]),
                             (b_kv[:], t["b_kv"].to_broadcast([P, RANK])),
                             (b_o[:], t["b_o"].to_broadcast([P, DIM]))):
                sp.dma_start(dst, src).then_inc(w_loaded, 16)
            sp.dma_start(x_t[:], t["xT"][:, :, 0:SEQ]).then_inc(xt_loaded, 16)
            sp.dma_start(x_tok[:], t["x"][0]).then_inc(x_loaded, 16)
            sp.wait_ge(wq_hi_set, 1)
            sp.wait_ge(wq_lo_set, 1)
            for m in range(2):
                sp.dma_start(wq_stage[:, m].bitcast(F32), wq_split[:, m].bitcast(F32)).then_inc(staged[m], 16)

            def batch(b, more):
                if more:
                    sp.wait_ge(proj[4], sp.snap(b + 1))
                    sp.dma_start(x_t[:], t["xT"][:, :, bass.ds((b + 1) * SEQ, SEQ)]).then_inc(xt_loaded, 16)
                    sp.wait_ge(xb_set, sp.snap(b + 1))
                    sp.dma_start(x_tok[:], t["x"][b + 1]).then_inc(x_loaded, 16)
                with sp.Fori(1, PAIRS // 2) as i:
                    for m in range(2):
                        sp.wait_ge(qproj[2], sp.snap(b * PAIRS + 2 * i + m + 1))
                        sp.dma_start(wq_stage[:, m].bitcast(F32), wq_split[:, 2 * i + m].bitcast(F32)).then_inc(staged[m], 16)
                if more:
                    for m in range(2):
                        sp.wait_ge(qproj[2], sp.snap(b * PAIRS + PAIRS + m + 1))
                        sp.dma_start(wq_stage[:, m].bitcast(F32), wq_split[:, m].bitcast(F32)).then_inc(staged[m], 16)
                sp.wait_ge(x1_set, sp.snap(b + 1))
                sp.dma_start(x1_dram[b], x1[:].rearrange("p t d -> p (t d)")).then_inc(x1_stored, 16)

            with sp.Fori(0, BATCH - 1) as b:
                batch(b, True)
            batch(BATCH - 1, False)
            sp.wait_ge(x1_stored, 16 * BATCH + 16)

            for dst, src in ((raw_in, t["w_in"]), (raw_sh, t["w_sh"]), (raw_out, t["w_out"]),
                             (w_g[:], t["w_g"]), (b_g[:], t["b_g"].to_broadcast([P, EXPERTS])),
                             (b_pre[:], t["b_pre"]), (b_up[:], t["b_up"]), (b_down[:], t["b_down"]),
                             (sel_raw, t["sel"]),
                             (before[:], t["before"].to_broadcast([P, EXPERTS * EXPERTS]))):
                sp.dma_start(dst, src).then_inc(fw_loaded, 16)
            sp.dma_start(y_tok[:].rearrange("p t d -> p (t d)"), x1_dram[0]).then_inc(y_loaded, 16)
            sp.dma_start(y_res[:].rearrange("p t d -> p (t d)"), x1_dram[0]).then_inc(y_res_loaded, 16)

            def ff_batch(b, more):
                if more:
                    sp.wait_ge(y_turned, sp.snap(b + 1))
                    sp.dma_start(y_tok[:].rearrange("p t d -> p (t d)"), x1_dram[b + 1]).then_inc(y_loaded, 16)
                    sp.wait_ge(z2_set[TT - 1], sp.snap(b + 2))
                    sp.dma_start(y_res[:].rearrange("p t d -> p (t d)"), x1_dram[b + 1]).then_inc(y_res_loaded, 16)
                sp.wait_ge(out_set, sp.snap(b + 1))
                sp.dma_start(out[b], x1[:]).then_inc(stored, 16)

            with sp.Fori(0, BATCH - 1) as b:
                ff_batch(b, True)
            ff_batch(BATCH - 1, False)
            sp.wait_ge(stored, 16 * BATCH + 16)

        @block.tensor
        def _(pe):
            pe.wait_ge(w_loaded, 16 * 14)
            for h in range(HEADS):
                mm = pe.matmul(bank[h // 8][:, (h % 8) * 64:(h % 8) * 64 + 64], wqn[:, h], wkn[:, h],
                               start=True, stop=True)
            mm.then_inc(m_made, 1)
            for h in range(HEADS):
                r = 64 if h % 2 == 0 else 0
                mm = pe.matmul(bank[2][r:r + 64, h:h + 1], wkn[:, h], b_qn[:, h:h + 1], start=True, stop=True)
            mm.then_inc(m_made, 1)
            for h in range(HEADS):
                a = h // 2
                r = 64 * (h % 2)
                mm = pe.matmul(bank[3 + a // 2][r:r + 64, (a % 2) * DIM:(a % 2) * DIM + DIM], wv[:, h], wo[:, h],
                               start=True, stop=True)
            mm.then_inc(g_made, 1)
            pe.wait_ge(bv_wide_set, 1)
            for h in range(HEADS):
                mm = pe.matmul(bank[7][:, 0:DIM], bv_wide[:, h], wo[:, h], start=(h == 0), stop=(h == HEADS - 1))
            mm.then_inc(g_made, 1)
            pe.wait_ge(wq_full, 1)
            pe.wait_ge(attn_w_set, 3)

            with pe.Fori(0, BATCH) as b:
                b1 = pe.snap(b + 1)
                b2 = pe.snap(b + 2)
                pe.wait_ge(xt_loaded, pe.snap(16 * b + 16))
                for c, dst in enumerate((s_bank[0], s_bank[1], pt_bank[0], pt_bank[1])):
                    for d in range(DC):
                        mm = pe.matmul(dst[:], w_a[:, d, c], x_t[:, d], start=(d == 0), stop=(d == DC - 1))
                    mm.then_inc(proj[c], 1)
                for k in range(TT):
                    for d in range(DC):
                        mm = pe.matmul(u_bank[:, k * RANK:(k + 1) * RANK], x_t[:, d, k * P:(k + 1) * P],
                                       w_a[:, d, 1, ROPE:P], start=(d == 0), stop=(d == DC - 1))
                mm.then_inc(proj[4], 1)

                def step(T, S, Q):
                    if Q is not None and S is None:
                        pe.wait_ge(cq_set, b1)
                        for i in range(1, TT):
                            pe.wait_ge(z_set[i], b1)
                    for j in range(TILES):
                        h, qt = divmod(j, TT)
                        if T is not None:
                            kt = j % TT
                            if kt == 0:
                                pe.wait_ge(probs_set[h], T.n1)
                            if j >= 2:
                                pe.wait_ge(pt_set[j - 2], T.n1)
                            else:
                                pe.wait_ge(pt_set[6 + j], T.n1)
                            for q in range(TT):
                                mm = pe.transpose(pt_bank[j % 2][:, q * P:(q + 1) * P],
                                                  probs[:, T.buf, h * TT + q, kt * P:(kt + 1) * P], ident[:])
                            mm.then_inc(turned[j], 1)
                        if S is not None:
                            if j == 0:
                                pe.wait_ge(q_hi_set, S.n1)
                                pe.wait_ge(q_lo_set, S.n1)
                                pe.wait_ge(k_hi_set, b1)
                                pe.wait_ge(k_lo_set, b1)
                            pe.wait_ge(exp_done[(j - 2) % TILES], S.n1)
                            cols = slice(qt * P, (qt + 1) * P)
                            pe.matmul(s_bank[j % 2][:], q_hi[:, S.buf, h, cols], k_hi[:, h], start=True, stop=False)
                            pe.matmul(s_bank[j % 2][:], q_hi[:, S.buf, h, cols], k_lo[:, h], start=False, stop=False)
                            pe.matmul(s_bank[j % 2][:], q_lo[:, S.buf, h, cols], k_hi[:, h], start=False,
                                      stop=True).then_inc(scores[j], 1)
                        if Q is not None and 1 <= j <= 3:
                            c = j - 1
                            if c == 0:
                                if Q.buf == 0:
                                    half = pe.snap((b * PAIRS + Q.pair) * 8 + 16)
                                else:
                                    half = pe.snap((b * PAIRS + Q.pair) * 8 + 8)
                                pe.wait_ge(staged[Q.buf], half)
                            for s in range(2):
                                mm = pe.matmul(q_bank[c][:], wq_stage[:, Q.buf, s, c * P:(c + 1) * P], cq[:],
                                               start=(s == 0), stop=(s == 1))
                            mm.then_inc(qproj[c], 1)
                        if T is not None and j >= TT:
                            kt = j - TT
                            pe.wait_ge(pt_set[kt], T.n1)
                            pe.wait_ge(pt_set[TT + kt], T.n1 if kt < 2 else T.n2)
                            if kt == 0:
                                pe.wait_ge(v_set, b1)
                                pe.wait_ge(u_set, T.n1)
                            for h2 in range(2):
                                mm = pe.matmul(u_bank[64 * h2:64 * h2 + 64, :], v_lat[:, kt], probs_t[:, h2 * TT + kt],
                                               start=(kt == 0), stop=(kt == TT - 1))
                            mm.then_inc(pv[kt], 1)

                walk(pe, b, step)
                pe.wait_ge(u_set, pe.snap(b * PAIRS + PAIRS + 1))
                for q in range(TT):
                    if q == 3:
                        pe.wait_ge(z_set[0], b2)
                    dst = q_bank[q % 3][:, 0:DIM]
                    cols = slice(q * P, (q + 1) * P)
                    for a in range(PAIRS):
                        pe.matmul(dst, u_hi[:, a, cols], g_hi[:, a], start=(a == 0), stop=False)
                        pe.matmul(dst, u_hi[:, a, cols], g_lo[:, a], start=False, stop=False)
                        mm = pe.matmul(dst, u_lo[:, a, cols], g_hi[:, a], start=False, stop=(a == PAIRS - 1))
                    mm.then_inc(oproj[q], 1)

            pe.wait_ge(fw_loaded, 160)
            pe.wait_ge(fw_hi_set, 4)
            pe.wait_ge(fw_lo_set, 3)
            for i in range(TT):
                pe.wait_ge(z_set[i], BATCH + 1)
            with pe.Fori(0, BATCH) as b:
                b1 = pe.snap(b + 1)
                at = [pe.snap(b * (UNITS // 2) + k) for k in range(UNITS // 2 + 2)]
                at_e = [pe.snap(b * (ROUTED // 2) + k) for k in range(ROUTED // 2 + 1)]
                b2 = pe.snap(b + 2)
                pe.wait_ge(y_loaded, pe.snap(16 * b + 16))
                pe.wait_ge(h_lo_set[0], at[1])
                pe.wait_ge(h_lo_set[1], at[1])
                for d in range(DC):
                    for q in range(TT):
                        mm = pe.transpose(bank[d][:, q * P:(q + 1) * P], y_tok[:, q, d * P:(d + 1) * P], ident[:])
                mm.then_inc(y_turned, 1)
                pe.wait_ge(y_raw_set, b1)
                pe.wait_ge(z2_set[2], b1)
                for q in range(TT):
                    for d in range(DC):
                        mm = pe.matmul(bank[6][:, q * EXPERTS:(q + 1) * EXPERTS], y_raw[:, d, q * P:(q + 1) * P],
                                       w_g[:, d], start=(d == 0), stop=(d == DC - 1))
                mm.then_inc(routed, 1)
                pe.wait_ge(y_hi_set, b1)
                pe.wait_ge(y_lo_set, b1)

                def product(dst, w, d_w):
                    for d in range(DC):
                        pe.matmul(dst, w[:, 0, d, d_w], y_hi[:, d], start=(d == 0), stop=False)
                        pe.matmul(dst, w[:, 1, d, d_w], y_hi[:, d], start=False, stop=False)
                        mm = pe.matmul(dst, w[:, 0, d, d_w], y_lo[:, d], start=False, stop=(d == DC - 1))
                    return mm

                def widen(u):
                    if u >= SHARED + 2:
                        pe.wait_ge(h_set[u % 2], at[u // 2])
                    for s in range(2):
                        mm = pe.matmul(bank[4 + u % 2][:], sel[:, u - SHARED], w_t_split[:, s],
                                       start=(s == 0), stop=(s == 1))
                    mm.then_inc(widened[u % 2], 1)

                for u in range(UNITS):
                    if u >= 2:
                        pe.wait_ge(half_set[u % 2], at[u // 2])
                    if u >= SHARED + 2:
                        pe.wait_ge(gated[u % 2], at_e[u // 2 - 1])
                    if u < SHARED:
                        product(bank[u % 2][:], w_sh_v, u).then_inc(pre[u % 2], 1)
                    else:
                        product(bank[u % 2][:], w_in_v, u - SHARED)
                        product(bank[2 + u % 2][:], w_in_v, ROUTED + u - SHARED).then_inc(pre[u % 2], 1)
                    if u == 2:
                        pe.wait_ge(route_step, pe.snap(ROUTE_STEPS * b + ROUTE_STEPS))
                        pe.wait_ge(z2_set[3], b1)
                        for q in range(TT):
                            mm = pe.transpose(bank[7][0:EXPERTS, q * P:(q + 1) * P], w_tok[:, q], ident[:])
                        mm.then_inc(w_turned, 1)
                    if u == 3:
                        pe.wait_ge(w_hi_set, b1)
                        pe.wait_ge(w_lo_set, b1)
                        widen(2)
                        widen(3)
                    if u > 3:
                        widen(u)
                for q in range(TT):
                    dst = bank[6 + q % 2][:, 0:DIM]
                    cols = slice(q * P, (q + 1) * P)
                    if q >= 2:
                        pe.wait_ge(z2_set[q - 2], b2)
                    pe.matmul(dst, w_t[:, cols], b_down[:], start=True, stop=False)
                    for u in range(UNITS):
                        if q == 0:
                            pe.wait_ge(h_hi_set[u % 2], at[u // 2 + 1])
                            pe.wait_ge(h_lo_set[u % 2], at[u // 2 + 2])
                        pe.matmul(dst, h_hi[:, u, cols], w_out_hi[:, u], start=False, stop=False)
                        pe.matmul(dst, h_hi[:, u, cols], w_out_lo[:, u], start=False, stop=False)
                        mm = pe.matmul(dst, h_lo[:, u, cols], w_out_hi[:, u], start=False, stop=(u == UNITS - 1))
                    mm.then_inc(down[q], 1)

        @block.scalar
        def _(act):
            act.wait_ge(m_made, 1)
            act.wait_ge(w_loaded, 16 * 14)
            for k in range(2):
                m4 = bank[k][:].rearrange("p (a s j) -> p a s j", s=2, j=64)
                act.copy(wq_raw[:, 4 * k:4 * k + 4, 0, 64:128], m4[:, :, 0, :])
                last = act.copy(wq_raw[:, 4 * k:4 * k + 4, 1, 0:64], m4[:, :, 1, :])
            last.then_inc(wq_full, 1)
            act.wait_ge(wq_full, 1)
            act.copy(wq_split[:, :, 0, :], wq_raw.rearrange("p a c m -> p a (c m)")).then_inc(wq_hi_set, 1)
            act.wait_ge(g_made, 1)
            for k in range(4):
                act.copy(g_hi[:, 2 * k:2 * k + 2, :], bank[3 + k][:].rearrange("p (a n) -> p a n", a=2))\
                   .then_inc(g_hi_set, 1)

            with act.Fori(0, BATCH) as b:
                b1 = act.snap(b + 1)
                act.wait_ge(proj[0], b1)
                act.activation(cq_raw[:], s_bank[0][:], ACT.Identity, bias=b_a[:, 0:1]).then_inc(cq_raw_set, 1)
                act.wait_ge(cq_raw_set, b1)
                act.copy(cq[:], cq_raw[:]).then_inc(cq_hi_set, 1)
                act.wait_ge(k_full, act.snap(2 * b + 2))
                act.copy(k_hi[:], roped[:]).then_inc(k_hi_set, 1)

                def step(T, S, Q):
                    def exp(j):
                        act.wait_ge(rowmax[j], S.n1)
                        act.activation(probs[:, S.buf, j], s_bank[j % 2][:], ACT.Exp,
                                       bias=neg_max[:, S.buf, j:j + 1],
                                       accum_out=sums[:, S.buf, j:j + 1]).then_inc(exp_done[j], 1)
                    for j in range(TILES):
                        if T is not None:
                            act.wait_ge(turned[j], T.n1)
                            act.wait_ge(pv[j % TT], T.n1)
                            act.copy(probs_t[:, j], pt_bank[j % 2][:]).then_inc(pt_set[j], 1)
                        if S is not None and j >= 1:
                            exp(j - 1)
                        if Q is not None and j == 6:
                            act.wait_ge(q_added, Q.n1)
                            act.copy(q_hi[:, Q.buf], roped[:]).then_inc(q_hi_set, 1)
                    if S is not None:
                        exp(TILES - 1)
                    if T is not None:
                        act.wait_ge(pv[TT - 1], T.n2)
                        act.copy(u_hi[:, T.pair], u_bank[:]).then_inc(u_hi_set, 1)

                walk(act, b, step)

            act.wait_ge(fw_loaded, 160)
            act.copy(wq_split[:].rearrange(flat)[:, 0:n_in], raw_in).then_inc(fw_hi_set, 1)
            act.copy(wq_stage[:].rearrange(flat)[:, 0:n_sh], raw_sh).then_inc(fw_hi_set, 1)
            act.copy(w_out_hi[:], raw_out).then_inc(fw_hi_set, 1)
            act.copy(sel, sel_raw).then_inc(fw_hi_set, 1)
            act.wait_ge(b_half_set, 1)
            with act.Fori(0, BATCH) as b:
                b1 = act.snap(b + 1)
                at = [act.snap(b * (UNITS // 2) + k) for k in range(UNITS // 2 + 2)]
                at_e = [act.snap(b * (ROUTED // 2) + k) for k in range(ROUTED // 2 + 1)]
                act.wait_ge(y_turned, b1)
                act.copy(y_raw[:, 0], bank[0][:])
                act.copy(y_raw[:, 1], bank[1][:]).then_inc(y_raw_set, 1)
                act.wait_ge(y_raw_set, b1)
                act.copy(y_hi[:], y_raw[:]).then_inc(y_hi_set, 1)

                def split_hi(u):
                    act.wait_ge(h_set[u % 2], at[u // 2 + 1])
                    act.copy(h_hi[:, u], hidden[:, u % 2]).then_inc(h_hi_set[u % 2], 1)

                for u in range(UNITS):
                    act.wait_ge(pre[u % 2], at[u // 2 + 1])
                    if u >= SHARED + 2:
                        act.wait_ge(silu_set[u % 2], at_e[u // 2 - 1])
                    act.activation(half_pre[:, u % 2], bank[u % 2][:], ACT.Identity, bias=b_pre[:, u:u + 1],
                                   scale=0.5).then_inc(half_set[u % 2], 1)
                    act.wait_ge(half_set[u % 2], at[u // 2 + 1])
                    act.activation(tanh_pre[:, u % 2], half_pre[:, u % 2], ACT.Tanh).then_inc(tanh_set[u % 2], 1)
                    if u == 0:
                        act.wait_ge(route_step, act.snap(ROUTE_STEPS * b + ROUTE_EXP))
                        act.activation(odds[:], shifted[:], ACT.Exp).then_inc(odds_set, 1)
                    if u >= 1:
                        split_hi(u - 1)
                    if u == 2:
                        act.wait_ge(w_turned, b1)
                        act.copy(w_t, bank[7][0:EXPERTS, :]).then_inc(w_t_set, 1)
                        act.wait_ge(w_t_set, b1)
                        act.copy(w_t_split[:, 0], w_t).then_inc(w_hi_set, 1)
                split_hi(UNITS - 1)

        @block.vector
        def _(dve):
            dve.memset(ones[:], 1.0).then_inc(consts_set, 1)
            dve.wait_ge(w_loaded, 16 * 14)
            dve.wait_ge(consts_set, 1)
            for h in range(HEADS):
                last = dve.tensor_scalar(bv_wide[:, h], ones[:], b_v[:, h:h + 1], None, ALU.mult)
            last.then_inc(bv_wide_set, 1)
            dve.wait_ge(m_made, 2)
            bm = bank[2][:, 0:HEADS].rearrange("p (a s) -> p a s", s=2)
            dve.tensor_copy(b_q[64:128, :, 0], bm[64:128, :, 0])
            dve.tensor_copy(b_q[0:64, :, 1], bm[0:64, :, 1]).then_inc(attn_w_set, 1)
            dve.wait_ge(wq_hi_set, 1)
            dve.tensor_tensor(wq_split[:, :, 1, :], wq_raw.rearrange("p a c m -> p a (c m)"),
                              wq_split[:, :, 0, :].bitcast(F32), ALU.subtract).then_inc(wq_lo_set, 1)
            for k in range(4):
                dve.wait_ge(g_hi_set, k + 1)
                last = dve.tensor_tensor(g_lo[:, 2 * k:2 * k + 2, :], bank[3 + k][:].rearrange("p (a n) -> p a n", a=2),
                                         g_hi[:, 2 * k:2 * k + 2, :].bitcast(F32), ALU.subtract)
            last.then_inc(attn_w_set, 1)
            dve.wait_ge(g_made, 2)
            dve.tensor_tensor(b_o[:], bank[7][:, 0:DIM], b_o[:], ALU.add).then_inc(attn_w_set, 1)
            dve.memset(minus_half[:], -0.5).then_inc(consts_set, 1)

            with dve.Fori(0, BATCH) as b:
                b1 = dve.snap(b + 1)
                dve.wait_ge(cq_hi_set, b1)
                dve.tensor_tensor(cq[64:128], cq_raw[64:128], cq[64:128].bitcast(F32), ALU.subtract)\
                   .then_inc(cq_set, 1)
                for c, (src, dst) in enumerate(((s_bank[1], roped[:, 0]), (pt_bank[0], roped[:, 1]),
                                                (pt_bank[1], rot[:]))):
                    dve.wait_ge(proj[c + 1], b1)
                    last = dve.scalar_tensor_tensor(out=dst, in0=src[:], scalar=b_a[:, c + 1:c + 2],
                                                    in1=rope[:, 3 + c], op0=ALU.add, op1=ALU.mult)
                last.then_inc(k_part, 1)
                dve.wait_ge(k_part, b1)
                dve.tensor_tensor(roped[0:64, 0], roped[0:64, 0], rot[0:64], ALU.add).then_inc(k_full, 1)
                dve.tensor_tensor(roped[64:128, 1], roped[64:128, 1], rot[64:128], ALU.add).then_inc(k_full, 1)
                dve.wait_ge(proj[4], b1)
                dve.tensor_tensor(v_lat[:], u_bank[:, 0:TT * RANK].rearrange("p (k r) -> p k r", k=TT),
                                  b_kv[:].rearrange("p (a r) -> p a r", a=1).to_broadcast([P, TT, RANK]), ALU.add)\
                   .then_inc(v_set, 1)
                dve.wait_ge(k_hi_set, b1)
                dve.tensor_tensor(k_lo[:], roped[:], k_hi[:].bitcast(F32), ALU.subtract).then_inc(k_lo_set, 1)

                dve.wait_ge(k_lo_set, b1)

                def step(T, S, Q):
                    def normalise(j):
                        dve.wait_ge(exp_done[j], S.n1 if j < 6 else S.n2)
                        dve.reciprocal(inv[:, S.buf, j:j + 1], sums[:, S.buf, j:j + 1]).then_inc(inv_set[j], 1)
                        dve.wait_ge(inv_set[j], S.n1)
                        op = dve.tensor_scalar(probs[:, S.buf, j], probs[:, S.buf, j], inv[:, S.buf, j:j + 1],
                                               None, ALU.mult)
                        if j % TT == TT - 1:
                            op.then_inc(probs_set[j // TT], 1)
                    for j in range(TILES):
                        if S is not None:
                            dve.wait_ge(scores[j], S.n1)
                            dve.tensor_reduce(neg_max[:, S.buf, j:j + 1], s_bank[j % 2][:], AX.X, ALU.max,
                                              negate=True).then_inc(rowmax[j], 1)
                            if j >= 1:
                                normalise(j - 1)
                        if Q is not None and 2 <= j <= 4:
                            c = j - 2
                            dve.wait_ge(qproj[c], Q.n1 if c < 2 else dve.snap(b * PAIRS + Q.pair + 3))
                            op = dve.scalar_tensor_tensor(out=roped[:, c] if c < 2 else rot[:], in0=q_bank[c][:],
                                                     scalar=b_q[:, Q.pair, c:c + 1], in1=rope[:, c],
                                                     op0=ALU.add, op1=ALU.mult)
                            if c == 2:
                                op.then_inc(q_cos, 1)
                    if S is not None:
                        normalise(TILES - 1)
                    if T is not None:
                        dve.wait_ge(u_hi_set, T.n1)
                        dve.tensor_tensor(u_lo[:, T.pair], u_bank[:], u_hi[:, T.pair].bitcast(F32), ALU.subtract)\
                           .then_inc(u_set, 1)

                walk(dve, b, step)
                dve.wait_ge(xb_set, b1)
                for q in range(TT):
                    dve.wait_ge(oproj[q], b1)
                    dve.tensor_tensor(z[:, q], q_bank[q % 3][:, 0:DIM], x_b[:, q], ALU.add).then_inc(z_set[q], 1)
                b2 = dve.snap(b + 2)
                for q in range(TT):
                    dve.wait_ge(z_set[q], b2)
                    if q >= 1:
                        dve.wait_ge(stats_set, dve.snap(TT * b + q))
                    dve.bn_stats(stats[:, q], z[:, q]).then_inc(stats_set, 1)
                    if q >= 1:
                        last = dve.bn_aggr(mv[:, q - 1], stats[:, q - 1])
                last.then_inc(mv_set, 1)
                dve.wait_ge(stats_set, dve.snap(TT * b + TT))
                dve.wait_ge(mv_set, dve.snap(2 * b + 1))
                dve.tensor_scalar(var_e[:, 0:TT - 1], mv[:, 0:TT - 1, 1], EPS, None, ALU.add)
                dve.bn_aggr(mv[:, TT - 1], stats[:, TT - 1]).then_inc(mv_set, 1)
                dve.wait_ge(mv_set, dve.snap(2 * b + 2))
                dve.tensor_scalar(var_e[:, TT - 1:], mv[:, TT - 1:, 1], EPS, None, ALU.add)\
                   .then_inc(var_set, 1)
                dve.wait_ge(rstd_set, b1)
                dve.wait_ge(x1_stored, dve.snap(16 * b + 16))
                for q in range(TT):
                    last = dve.tensor_scalar(x1[:, q], z[:, q], mv[:, q, 0:1], rstd[:, q:q + 1],
                                             ALU.subtract, ALU.mult)
                last.then_inc(x1_set, 1)

            dve.wait_ge(fw_loaded, 160)
            dve.tensor_scalar(b_pre[:], b_pre[:], 0.5, None, ALU.mult).then_inc(b_half_set, 1)
            dve.memset(w_tok[:], 0.0).then_inc(fw_const, 1)
            dve.wait_ge(fw_const, 1)
            dve.memset(w_tok[:, :, ROUTED:ROUTED + 1], 1.0).then_inc(fw_const, 1)
            for n, (lo, raw, hi) in enumerate((
                    (wq_split[:].rearrange(flat)[:, n_in:2 * n_in], raw_in, wq_split[:].rearrange(flat)[:, 0:n_in]),
                    (wq_stage[:].rearrange(flat)[:, n_sh:2 * n_sh], raw_sh, wq_stage[:].rearrange(flat)[:, 0:n_sh]),
                    (w_out_lo[:], raw_out, w_out_hi[:]))):
                dve.wait_ge(fw_hi_set, n + 1)
                dve.tensor_tensor(lo, raw, hi.bitcast(F32), ALU.subtract).then_inc(fw_lo_set, 1)
            dve.wait_ge(fw_const, 2)
            with dve.Fori(0, BATCH) as b:
                b1 = dve.snap(b + 1)
                at = [dve.snap(b * (UNITS // 2) + k) for k in range(UNITS // 2 + 2)]
                at_e = [dve.snap(b * (ROUTED // 2) + k) for k in range(ROUTED // 2 + 1)]
                b2 = dve.snap(b + 2)
                dve.wait_ge(y_hi_set, b1)
                dve.tensor_tensor(y_lo[:], y_raw[:], y_hi[:].bitcast(F32), ALU.subtract).then_inc(y_lo_set, 1)

                steps = [0]

                def then(ins):
                    steps[0] += 1
                    ins.then_inc(route_step, 1)
                    dve.wait_ge(route_step, dve.snap(ROUTE_STEPS * b + steps[0]))
                dve.wait_ge(routed, b1)
                e3 = [P, TT, EXPERTS]
                then(dve.tensor_tensor(gate[:], bank[6][:, 0:TT * EXPERTS].rearrange("p (t e) -> p t e", t=TT),
                                       b_g[:].rearrange("p (a e) -> p a e", a=1).to_broadcast(e3), ALU.add))
                then(dve.tensor_reduce(top[:], gate[:], AX.X, ALU.max, negate=True))
                then(dve.tensor_tensor(shifted[:], gate[:],
                                       top[:].rearrange("p (t a) -> p t a", a=1).to_broadcast(e3), ALU.add))
                assert steps[0] == ROUTE_EXP
                other = gate[:].rearrange("p t (a f) -> p t a f", a=1).to_broadcast([P, TT, EXPERTS, EXPERTS])
                own = gate[:].rearrange("p t (e a) -> p t e a", a=1).to_broadcast([P, TT, EXPERTS, EXPERTS])
                then(dve.tensor_tensor(above, other, own, ALU.is_gt))
                then(dve.tensor_tensor(ties, other, own, ALU.is_equal))
                f3 = "p t e f -> p t (e f)"
                then(dve.tensor_tensor(ties.rearrange(f3), ties.rearrange(f3),
                                       before[:].rearrange("p (a e) -> p a e", a=1).to_broadcast([P, TT, 64]),
                                       ALU.mult))
                then(dve.tensor_tensor(above, above, ties, ALU.add))
                then(dve.tensor_reduce(rank[:], above, AX.X, ALU.add))
                then(dve.tensor_scalar(chosen[:], rank[:], float(ROUTED), None, ALU.is_lt))
                dve.wait_ge(odds_set, b1)
                then(dve.tensor_tensor(picked[:], odds[:], chosen[:], ALU.mult))
                then(dve.tensor_reduce(total[:], picked[:], AX.X, ALU.add))
                then(dve.reciprocal(inv_total[:], total[:]))
                then(dve.tensor_tensor(w_tok[:, :, 0:ROUTED], picked[:, :, 0:ROUTED],
                                       inv_total[:].rearrange("p (t a) -> p t a", a=1).to_broadcast([P, TT, ROUTED]),
                                       ALU.mult))
                assert steps[0] == ROUTE_STEPS

                for u in range(UNITS):
                    dve.wait_ge(tanh_set[u % 2], at[u // 2 + 1])
                    if u >= 2:
                        dve.wait_ge(h_hi_set[u % 2], at[u // 2])
                    dve.wait_ge(h_lo_set[u % 2], at[u // 2 + 1])
                    op = dve.scalar_tensor_tensor(out=hidden[:, u % 2], in0=tanh_pre[:, u % 2], scalar=1.0,
                                                  in1=half_pre[:, u % 2], op0=ALU.add, op1=ALU.mult)
                    if u < SHARED:
                        op.then_inc(h_set[u % 2], 1)
                        continue
                    op.then_inc(silu_set[u % 2], 1)
                    dve.wait_ge(silu_set[u % 2], at_e[u // 2])
                    dve.scalar_tensor_tensor(out=hidden[:, u % 2], in0=bank[2 + u % 2][:], scalar=b_up[:, u:u + 1],
                                             in1=hidden[:, u % 2], op0=ALU.add, op1=ALU.mult).then_inc(gated[u % 2], 1)
                    if u == SHARED:
                        dve.wait_ge(w_hi_set, b1)
                        dve.tensor_tensor(w_t_split[:, 1], w_t, w_t_split[:, 0].bitcast(F32), ALU.subtract)\
                           .then_inc(w_lo_set, 1)
                    dve.wait_ge(gated[u % 2], at_e[u // 2])
                    dve.wait_ge(widened[u % 2], at_e[u // 2])
                    dve.tensor_tensor(hidden[:, u % 2], bank[4 + u % 2][:], hidden[:, u % 2], ALU.mult)\
                       .then_inc(h_set[u % 2], 1)
                dve.wait_ge(y_res_loaded, dve.snap(16 * b + 16))
                for q in range(TT):
                    dve.wait_ge(down[q], b1)
                    dve.tensor_tensor(z[:, q], bank[6 + q % 2][:, 0:DIM], y_res[:, q], ALU.add).then_inc(z2_set[q], 1)
                for q in range(TT):
                    dve.wait_ge(z2_set[q], b2)
                    if q >= 1:
                        dve.wait_ge(stats2_set, dve.snap(TT * b + q))
                    dve.bn_stats(stats[:, q], z[:, q]).then_inc(stats2_set, 1)
                    if q >= 1:
                        last = dve.bn_aggr(mv[:, q - 1], stats[:, q - 1])
                last.then_inc(mv2_set, 1)
                dve.wait_ge(stats2_set, dve.snap(TT * b + TT))
                dve.wait_ge(mv2_set, dve.snap(2 * b + 1))
                dve.tensor_scalar(var_e[:, 0:TT - 1], mv[:, 0:TT - 1, 1], EPS, None, ALU.add)
                dve.bn_aggr(mv[:, TT - 1], stats[:, TT - 1]).then_inc(mv2_set, 1)
                dve.wait_ge(mv2_set, dve.snap(2 * b + 2))
                dve.tensor_scalar(var_e[:, TT - 1:], mv[:, TT - 1:, 1], EPS, None, ALU.add)\
                   .then_inc(var2_set, 1)
                dve.wait_ge(rstd2_set, b1)
                dve.wait_ge(stored, dve.snap(16 * b + 16))
                for q in range(TT):
                    last = dve.tensor_scalar(x1[:, q], z[:, q], mv[:, q, 0:1], rstd[:, q:q + 1],
                                             ALU.subtract, ALU.mult)
                last.then_inc(out_set, 1)

        @block.gpsimd
        def _(pool):
            for s, n in [(z, 1) for z in z_set] + [(qproj[2], 2)] + [(s, 1) for s in exp_done[6:] + pt_set[6:] + pv]\
                    + [(u_set, 1)] + [(s, 1) for s in z2_set + h_lo_set] + [(stored, 16), (x1_stored, 16)]:
                pool.sem_inc(s, n)
            pool.wait_ge(attn_w_set, 3)
            pool.wait_ge(consts_set, 2)
            with pool.Fori(0, BATCH) as b:
                b1 = pool.snap(b + 1)
                pool.wait_ge(x_loaded, pool.snap(16 * b + 16))
                for i in range(TT):
                    last = pool.tensor_tensor(x_b[:, i], x_tok[:, i], b_o[:], ALU.add)
                last.then_inc(xb_set, 1)

                def step(T, S, Q):
                    if Q is None:
                        return
                    pool.wait_ge(q_cos, Q.n1)
                    pool.tensor_tensor(roped[0:64, 0], roped[0:64, 0], rot[0:64], ALU.add).then_inc(q_added0, 1)
                    pool.wait_ge(q_added0, Q.n1)
                    pool.tensor_tensor(roped[64:128, 1], roped[64:128, 1], rot[64:128], ALU.add).then_inc(q_added, 1)
                    pool.wait_ge(q_added, Q.n1)
                    pool.wait_ge(q_hi_set, Q.n1)
                    pool.tensor_tensor(q_lo[:, Q.buf], roped[:], q_hi[:, Q.buf].bitcast(F32), ALU.subtract)\
                        .then_inc(q_lo_set, 1)

                walk(pool, b, step)
                pool.wait_ge(var_set, b1)
                pool.tensor_tensor(rstd[:], var_e[:], minus_half[:], ALU.pow).then_inc(rstd_set, 1)

            with pool.Fori(0, BATCH) as b:
                b1 = pool.snap(b + 1)
                at = [pool.snap(b * (UNITS // 2) + k) for k in range(UNITS // 2 + 2)]
                for u in range(UNITS):
                    pool.wait_ge(h_hi_set[u % 2], at[u // 2 + 1])
                    pool.tensor_tensor(h_lo[:, u], hidden[:, u % 2], h_hi[:, u].bitcast(F32), ALU.subtract)\
                        .then_inc(h_lo_set[u % 2], 1)
                pool.wait_ge(var2_set, b1)
                pool.tensor_tensor(rstd[:], var_e[:], minus_half[:], ALU.pow).then_inc(rstd2_set, 1)


def layouts(inputs):
    g = {k.replace("L0_", ""): np.asarray(v) for k, v in inputs.items()}
    even, odd = np.arange(0, ROPE, 2), np.arange(1, ROPE, 2)
    pe, rt = np.concatenate([even, odd]), np.concatenate([odd, even])
    cat = np.concatenate
    x = g["attn_x"]
    o = {}
    o["x"] = x.reshape(BATCH, TT, P, DIM).transpose(0, 2, 1, 3)
    o["xT"] = x.reshape(BATCH * SEQ, DC, P).transpose(2, 1, 0)
    wqa, wkva = g["attn_wq_a_w"], g["attn_wkv_a_w"]
    kv, kpe, krt = wkva[:, :RANK], wkva[:, RANK + pe], wkva[:, RANK + rt]
    w_a = np.stack([cat([wqa, wqa], 1), cat([kpe, kv], 1), cat([kv, kpe], 1), cat([krt, krt], 1)], 1)
    o["w_a"] = w_a.reshape(DC, P, 4, P).transpose(1, 0, 2, 3)
    bqa, bkva = g["attn_wq_a_b"], g["attn_wkv_a_b"]
    bkv, bpe, brt = bkva[:RANK], bkva[RANK + pe], bkva[RANK + rt]
    o["b_a"] = np.stack([cat([bqa, bqa]), cat([bpe, bkv]), cat([bkv, bpe]), cat([brt, brt])], 1)
    o["b_kv"] = bkv[None]
    wqb = g["attn_wq_b_w"].reshape(RANK, HEADS, NOPE + ROPE)
    bqb = g["attn_wq_b_b"].reshape(HEADS, NOPE + ROPE)
    wkvb = g["attn_wkv_b_w"].reshape(RANK, HEADS, NOPE + VHD)
    bkvb = g["attn_wkv_b_b"].reshape(HEADS, NOPE + VHD)
    qn = wqb[:, :, :NOPE].transpose(2, 1, 0)
    o["wqn"] = cat([qn, qn], 2)
    o["wkn"] = wkvb[:, :, :NOPE].transpose(2, 1, 0)
    o["wv"] = wkvb[:, :, NOPE:].transpose(2, 1, 0)
    o["wo"] = g["attn_wo_w"].reshape(HEADS, VHD, DIM).transpose(1, 0, 2)
    o["b_qn"] = bqb[:, :NOPE].T
    o["b_v"] = bkvb[:, NOPE:].T
    o["b_o"] = g["attn_wo_b"][None]
    raw = np.zeros((P, PAIRS, 3, P), np.float32)
    b_q = np.zeros((P, PAIRS, 4), np.float32)
    for r in (slice(0, 64), slice(64, 128)):
        raw[r, :, 0, 0:64] = wqb[:, 0::2, NOPE + pe]
        raw[r, :, 1, 64:128] = wqb[:, 1::2, NOPE + pe]
        raw[r, :, 2, 0:64] = wqb[:, 0::2, NOPE + rt]
        raw[r, :, 2, 64:128] = wqb[:, 1::2, NOPE + rt]
    b_q[0:64, :, 0] = bqb[0::2, NOPE + pe].T
    b_q[64:128, :, 1] = bqb[1::2, NOPE + pe].T
    b_q[0:64, :, 2] = bqb[0::2, NOPE + rt].T
    b_q[64:128, :, 2] = bqb[1::2, NOPE + rt].T
    o["wq_raw"], o["b_q"] = raw, b_q
    def cols(w):
        return w.reshape(-1, DC, P, HID).transpose(2, 1, 0, 3)
    ws = g["ffn_Ws_up"].reshape(DIM, SHARED, HID).transpose(1, 0, 2)
    o["w_in"] = cols(cat([g["ffn_Wgate"], g["ffn_Wup"]], 0)).reshape(P, -1)
    o["w_sh"] = cols(ws).reshape(P, -1)
    o["w_out"] = cat([g["ffn_Ws_down"].reshape(SHARED, HID, DIM), g["ffn_Wdown"]], 0).transpose(1, 0, 2)
    o["w_g"] = g["ffn_Wg"].reshape(DC, P, EXPERTS).transpose(1, 0, 2)
    o["b_g"] = g["ffn_bg"][None]
    o["b_pre"] = cat([g["ffn_bs_up"].reshape(SHARED, HID), g["ffn_bgate"]], 0).T
    o["b_up"] = cat([np.zeros((SHARED, HID), np.float32), g["ffn_bup"]], 0).T
    o["b_down"] = cat([g["ffn_bdown"], g["ffn_bs_down"][None], np.zeros((1, DIM), np.float32)], 0)
    sel = np.zeros((EXPERTS, ROUTED, P), np.float32)
    for u in range(ROUTED):
        sel[u, u] = 1
    o["sel"] = sel
    o["before"] = np.tril(np.ones((EXPERTS, EXPERTS), np.float32), -1).reshape(1, -1)
    f = np.float32
    inv_freq = (f(1.0) / np.power(f(THETA), np.arange(0, ROPE, 2, dtype=f) / f(ROPE))).astype(f)
    ang = np.outer(np.arange(SEQ, dtype=f), inv_freq).astype(f)
    c, s = np.cos(ang).T.astype(f), np.sin(ang).T.astype(f)
    cc, ss, one = cat([c, c]), cat([-s, s]), np.ones((64, SEQ), f)
    tabs = [cat([cc, one]), cat([one, cc]), cat([ss, ss])]
    o["rope"] = np.stack(tabs + [(a * f(SCALE)).astype(f) for a in tabs], 1)
    o["ident"] = np.eye(P, dtype=f)
    return {k: np.ascontiguousarray(v) for k, v in o.items()}


def kernel(**inputs):
    import concourse.bacc as bacc
    from concourse.bass_utils import run_bass_kernel_spmd

    nc = bacc.Bacc("TRN2", target_bir_lowering=False, num_devices=1)
    arrays, t = {}, {}
    for name, a in layouts(inputs).items():
        arrays[f"in_{name}"] = a
        t[name] = nc.dram_tensor(f"in_{name}", a.shape, mybir.dt.from_np(a.dtype), kind="ExternalInput").ap()
    out = nc.dram_tensor("out", (BATCH, SEQ, DIM), F32, kind="ExternalOutput").ap()
    program(nc, t, out.rearrange("b (t p) d -> b p t d", p=P))
    r = run_bass_kernel_spmd(nc, [arrays], core_ids=[0])
    return np.asarray(r.results[0]["out"])
```

```python
from contextlib import ExitStack

import numpy as np
import concourse.bass as bass
from concourse import mybir

F32 = mybir.dt.float32
F32R = mybir.dt.float32r
ALU = mybir.AluOpType
ACT = mybir.ActivationFunctionType
AX = mybir.AxisListType

P = 128
BATCH, SEQ, DIM = 8, 512, 256
HEADS, NOPE, ROPE, VHD = 16, 128, 64, 128
RANK = 64
PAIRS = HEADS // 2
DC = DIM // P
TT = SEQ // P
EXPERTS, ROUTED, HID = 8, 6, 128
SHARED = 2
UNITS = ROUTED + SHARED
EPS = 1e-5
THETA = 1000000.0
SCALE = 1.0 / float(np.sqrt(VHD))
TILES = 2 * TT
ROUTE_STEPS, ROUTE_EXP = 13, 3


def program(nc, t, out):
    ctx = ExitStack()
    with ctx:
        def sb(name, shape, dt=F32):
            return ctx.enter_context(nc.sbuf_tensor(name, shape, dt))

        def sem(name):
            return ctx.enter_context(nc.semaphore(name))

        def sems(name, n):
            return [sem(f"{name}{i}") for i in range(n)]

        x1_dram = nc.dram_tensor("x1_scratch", (BATCH, P, TT * DIM), F32, kind="Internal").ap()

        bank = [ctx.enter_context(nc.psum_tensor(f"bank{i}", [P, 512], F32)) for i in range(8)]
        s_bank, pt_bank, q_bank, u_bank = bank[0:2], bank[2:4], bank[4:7], bank[7]

        arena = sb("arena", [P, 13312])

        def view(at, n):
            return arena[:, at:at + n]
        wq_raw = view(0, 3072).rearrange("p (a c m) -> p a c m", a=PAIRS, c=3)
        wqn = view(3072, 2048).rearrange("p (h i) -> p h i", h=HEADS)
        wkn = view(5120, 1024).rearrange("p (h j) -> p h j", h=HEADS)
        wv = view(6144, 1024).rearrange("p (h j) -> p h j", h=HEADS)
        wo = view(7168, 4096).rearrange("p (h n) -> p h n", h=HEADS)
        bv_wide = view(11264, 2048).rearrange("p (h m) -> p h m", h=HEADS)
        probs = view(0, 8192).rearrange("p (m j k) -> p m j k", m=2, j=TILES)
        probs_t = view(8192, 4096).rearrange("p (k q) -> p k q", k=TILES)

        ident = sb("ident", [P, P])
        rope = sb("rope", [P, 3, SEQ])
        w_a = sb("w_a", [P, DC, 4, P])
        b_a = sb("b_a", [P, 4])
        b_kv = sb("b_kv", [P, RANK])
        b_qn = sb("b_qn", [P, HEADS])
        b_v = sb("b_v", [P, HEADS])
        b_o = sb("b_o", [P, DIM])
        b_q = sb("b_q", [P, PAIRS, 4])
        ones = sb("ones", [P, P])
        wq_split = sb("wq_split", [P, PAIRS, 2, 3 * P], F32R)
        wq_stage = sb("wq_stage", [P, 2, 2, 3 * P], F32R)
        g_hi = sb("g_hi", [P, PAIRS, DIM], F32R)
        g_lo = sb("g_lo", [P, PAIRS, DIM], F32R)
        x_t = sb("x_t", [P, DC, SEQ])
        x_tok = sb("x_tok", [P, TT, DIM])
        x_b = sb("x_b", [P, TT, DIM])
        z = sb("z", [P, TT, DIM])
        x1 = sb("x1", [P, TT, DIM])
        stats = sb("stats", [P, TT, 6])
        mv = sb("mv", [P, TT, 2])
        var_e = sb("var_e", [P, TT])
        rstd = sb("rstd", [P, TT])
        minus_half = sb("minus_half", [P, TT])
        cq_raw = sb("cq_raw", [P, SEQ])
        cq = sb("cq", [P, SEQ], F32R)
        k_hi = sb("k_hi", [P, 2, SEQ], F32R)
        k_lo = sb("k_lo", [P, 2, SEQ], F32R)
        v_lat = sb("v_lat", [P, TT, RANK])
        k_rope = sb("k_rope", [P, 2, SEQ])
        v_next = sb("v_next", [P, TT, RANK])
        roped = sb("roped", [P, 2, SEQ])
        rot = sb("rot", [P, SEQ])
        q_hi = sb("q_hi", [P, 2, 2, SEQ], F32R)
        q_lo = sb("q_lo", [P, 2, 2, SEQ], F32R)
        neg_max = sb("neg_max", [P, 2, TILES])
        sums = sb("sums", [P, 2, TILES])
        inv = sb("inv", [P, 2, TILES])
        u_hi = sb("u_hi", [P, PAIRS, SEQ], F32R)
        u_lo = sb("u_lo", [P, PAIRS, SEQ], F32R)

        flat = "p a c m -> p (a c m)"
        n_in, n_sh = DC * 2 * ROUTED * HID, DC * SHARED * HID
        w_in_v = wq_split[:].rearrange("p a c m -> p (a c m)").rearrange(
            "p (s d u m) -> p s d u m", s=2, d=DC, u=2 * ROUTED)
        w_sh_v = wq_stage[:].rearrange("p a c m -> p (a c m)")[:, 0:2 * DC * SHARED * HID].rearrange(
            "p (s d u m) -> p s d u m", s=2, d=DC, u=SHARED)
        w_out_hi, w_out_lo = g_hi, g_lo
        h_hi, h_lo = u_hi, u_lo
        y_raw, y_hi, y_lo = roped, k_hi, k_lo
        y_tok, y_res = x_tok, x_b
        sel = q_hi[0:EXPERTS].rearrange("p a c m -> p (a c m)")[:, 0:ROUTED * P].rearrange(
            "p (u m) -> p u m", u=ROUTED)
        w_t_split = q_lo[0:EXPERTS, 0]
        raw_in = view(0, DC * 2 * ROUTED * HID)
        raw_sh = view(3072, DC * SHARED * HID)
        raw_out = view(4096, UNITS * DIM).rearrange("p (u n) -> p u n", u=UNITS)
        half_pre = view(6144, 2 * SEQ).rearrange("p (m q) -> p m q", m=2)
        tanh_pre = view(7168, 2 * SEQ).rearrange("p (m q) -> p m q", m=2)
        hidden = view(8192, 2 * SEQ).rearrange("p (m q) -> p m q", m=2)
        w_g = sb("w_g", [P, DC, EXPERTS])
        b_g = sb("b_g", [P, EXPERTS])
        b_pre = sb("b_pre", [P, UNITS])
        b_up = sb("b_up", [P, UNITS])
        b_down = sb("b_down", [EXPERTS, DIM])
        sel_raw = view(9216, ROUTED * P)[0:EXPERTS].rearrange("p (u m) -> p u m", u=ROUTED)
        before = sb("before", [P, EXPERTS * EXPERTS])
        gate = sb("gate", [P, TT, EXPERTS])
        above = view(9984, 256).rearrange("p (t e f) -> p t e f", t=TT, e=EXPERTS)
        ties = view(10240, 256).rearrange("p (t e f) -> p t e f", t=TT, e=EXPERTS)
        rank = sb("rank", [P, TT, EXPERTS])
        chosen = sb("chosen", [P, TT, EXPERTS])
        top = sb("top", [P, TT])
        shifted = sb("shifted", [P, TT, EXPERTS])
        odds = sb("odds", [P, TT, EXPERTS])
        picked = sb("picked", [P, TT, EXPERTS])
        total = sb("total", [P, TT])
        inv_total = sb("inv_total", [P, TT])
        w_tok = sb("w_tok", [P, TT, EXPERTS])
        w_t = view(10496, SEQ)[0:EXPERTS]

        w_loaded = sem("w_loaded")
        consts_set = sem("consts_set")
        bv_wide_set = sem("bv_wide_set")
        m_made = sem("m_made")
        g_made = sem("g_made")
        wq_full = sem("wq_full")
        wq_hi_set = sem("wq_hi_set")
        wq_lo_set = sem("wq_lo_set")
        g_hi_set = sem("g_hi_set")
        attn_w_set = sem("attn_w_set")
        xt_loaded, x_loaded = sem("xt_loaded"), sem("x_loaded")
        proj = sems("proj", 5)
        cq_raw_set, cq_hi_set, cq_set = sem("cq_raw_set"), sem("cq_hi_set"), sem("cq_set")
        k_read, k_full, k_hi_set, k_lo_set = sem("k_read"), sem("k_full"), sem("k_hi_set"), sem("k_lo_set")
        v_next_set, v_set = sem("v_next_set"), sem("v_set")
        xb_set = sem("xb_set")
        oproj = sems("oproj", TT)
        z_set = sems("z_set", TT)
        stats_set, mv_set, var_set, rstd_set, x1_set = (sem("stats_set"), sem("mv_set"), sem("var_set"),
                                                        sem("rstd_set"), sem("x1_set"))
        x1_stored = sem("x1_stored")
        staged = sems("staged", 2)
        qproj = sems("qproj", 3)
        q_cos = sem("q_cos")
        q_added0, q_added, q_hi_set, q_lo_set = sem("q_added0"), sem("q_added"), sem("q_hi_set"), sem("q_lo_set")
        q_hi0_set = sem("q_hi0_set")
        q_lo0_set = sem("q_lo0_set")
        scores = sems("scores", TILES)
        rowmax = sems("rowmax", TILES)
        exp_done = sems("exp_done", TILES)
        inv_set = sems("inv_set", TILES)
        probs_set = sems("probs_set", 2)
        turned = sems("turned", TILES)
        pt_set = sems("pt_set", TILES)
        pv = sems("pv", TT)
        u_hi_set = sem("u_hi_set")
        u_set = sem("u_set")

        small_loaded = sem("small_loaded")
        fw_late_loaded, out_lo_set = sem("fw_late_loaded"), sem("out_lo_set")
        fw_loaded, fw_const, fw_hi_set, fw_lo_set, b_half_set = (
            sem("fw_loaded"), sem("fw_const"), sem("fw_hi_set"), sem("fw_lo_set"), sem("b_half_set"))
        y_loaded, y_turned, y_raw_set, y_hi_set, y_lo_set, y_res_loaded = (
            sem("y_loaded"), sem("y_turned"), sem("y_raw_set"), sem("y_hi_set"), sem("y_lo_set"), sem("y_res_loaded"))
        routed = sem("routed")
        route_step = sem("route_step")
        odds_set, w_turned, w_t_set, w_hi_set, w_lo_set = (
            sem("odds_set"), sem("w_turned"), sem("w_t_set"), sem("w_hi_set"), sem("w_lo_set"))
        pre = sems("pre", 2)
        half_set = sems("half_set", 2)
        tanh_set = sems("tanh_set", 2)
        silu_set = sems("silu_set", 2)
        gated = sems("gated", 2)
        widened = sems("widened", 2)
        h_set = sems("h_set", 2)
        h_hi_set = sems("h_hi_set", 2)
        h_lo_set = sems("h_lo_set", 2)
        down = sems("down", TT)
        z2_set = sems("z2_set", TT)
        stored = sem("stored")

        block = ctx.enter_context(nc.Block())

        class Item:
            def __init__(self, eng, b, pair, buf):
                self.pair, self.buf = pair, buf
                self.b1 = eng.snap(b + 1)
                self.b0 = b
                self.n1 = eng.snap(b * PAIRS + pair + 1)
                self.n2 = eng.snap(b * PAIRS + pair + 2)

        def walk(eng, step, between, finish):
            step(None, None, Item(eng, 0, 0, 0), latents=True)
            between(0)
            step(None, Item(eng, 0, 0, 0), Item(eng, 0, 1, 1), values=True)

            def batch(b, more):
                with eng.Fori(0, PAIRS // 2 - 1) as i:
                    a0, a1, a2, a3 = [Item(eng, b, 2 * i + k, k % 2) for k in range(4)]
                    step(a0, a1, a2)
                    step(a1, a2, a3)
                last = Item(eng, b, PAIRS - 1, 1)
                if more:
                    nb = eng.snap(b + 1)
                    first = Item(eng, nb, 0, 0)
                    step(Item(eng, b, PAIRS - 2, 0), last, first, latents=True)
                    between(nb)
                    step(last, first, Item(eng, nb, 1, 1), values=True)
                else:
                    step(Item(eng, b, PAIRS - 2, 0), last, None)
                    step(last, None, None)
                finish(b, more)

            with eng.Fori(0, BATCH - 1) as b:
                batch(b, True)
            batch(BATCH - 1, False)

        @block.sync
        def _(sp):
            for dst, src in ((wqn, t["wqn"]), (wkn, t["wkn"]), (wv, t["wv"]), (wo, t["wo"]),
                             (wq_raw, t["wq_raw"]), (b_qn[:], t["b_qn"]), (b_v[:], t["b_v"]),
                             (b_q[:], t["b_q"]), (ident[:], t["ident"]), (b_a[:], t["b_a"]),
                             (w_a[:], t["w_a"]), (rope[:], t["rope"]),
                             (b_kv[:], t["b_kv"].to_broadcast([P, RANK])),
                             (b_o[:], t["b_o"].to_broadcast([P, DIM]))):
                sp.dma_start(dst, src).then_inc(w_loaded, 16)
            sp.dma_start(x_t[:], t["xT"][:, :, 0:SEQ]).then_inc(xt_loaded, 16)
            sp.dma_start(x_tok[:], t["x"][0]).then_inc(x_loaded, 16)
            for dst, src in ((w_g[:], t["w_g"]), (b_g[:], t["b_g"].to_broadcast([P, EXPERTS])),
                             (b_pre[:], t["b_pre"]), (b_up[:], t["b_up"]), (b_down[:], t["b_down"]),
                             (before[:], t["before"].to_broadcast([P, EXPERTS * EXPERTS]))):
                sp.dma_start(dst, src).then_inc(small_loaded, 16)
            sp.wait_ge(wq_hi_set, 1)
            sp.wait_ge(wq_lo_set, 1)

            def stage(b, pair, m):
                sp.wait_ge(qproj[2], sp.snap(b * PAIRS + pair + 1))
                sp.dma_start(wq_stage[:, m].bitcast(F32), wq_split[:, pair].bitcast(F32)).then_inc(staged[m], 16)
            for pair in range(4):
                stage(0, pair, pair % 2)

            def batch(b, more):
                if more:
                    sp.wait_ge(proj[4], sp.snap(b + 1))
                    sp.dma_start(x_t[:], t["xT"][:, :, bass.ds((b + 1) * SEQ, SEQ)]).then_inc(xt_loaded, 16)
                with sp.Fori(2, PAIRS // 2) as i:
                    for m in range(2):
                        stage(b, 2 * i + m, m)
                if more:
                    for pair in range(4):
                        stage(b + 1, pair, pair % 2)
                    sp.wait_ge(xb_set, sp.snap(b + 1))
                    sp.dma_start(x_tok[:], t["x"][b + 1]).then_inc(x_loaded, 16)
                else:
                    sp.wait_ge(xb_set, BATCH)
                    sp.wait_ge(x1_stored, 32)
                    sp.dma_start(y_tok[:].rearrange("p t d -> p (t d)"), x1_dram[0]).then_inc(y_loaded, 16)
                    sp.wait_ge(turned[TILES - 1], BATCH * PAIRS - 1)
                    sp.dma_start(raw_sh, t["w_sh"]).then_inc(fw_loaded, 16)
                    sp.dma_start(raw_in, t["w_in"]).then_inc(fw_loaded, 16)
                    sp.wait_ge(turned[TILES - 1], BATCH * PAIRS)
                    sp.dma_start(raw_out, t["w_out"]).then_inc(fw_late_loaded, 16)
                    sp.wait_ge(pv[TT - 1], BATCH * PAIRS + 1)
                    sp.dma_start(sel_raw, t["sel"]).then_inc(fw_late_loaded, 16)
                    sp.wait_ge(z_set[TT - 1], BATCH + 1)
                    sp.dma_start(y_res[:].rearrange("p t d -> p (t d)"), x1_dram[0]).then_inc(y_res_loaded, 16)
                sp.wait_ge(x1_set, sp.snap(b + 1))
                sp.dma_start(x1_dram[b], x1[:].rearrange("p t d -> p (t d)")).then_inc(x1_stored, 16)

            with sp.Fori(0, BATCH - 1) as b:
                batch(b, True)
            batch(BATCH - 1, False)
            sp.wait_ge(x1_stored, 16 * BATCH + 16)

            def ff_batch(b, more):
                if more:
                    sp.wait_ge(y_turned, sp.snap(b + 1))
                    sp.dma_start(y_tok[:].rearrange("p t d -> p (t d)"), x1_dram[b + 1]).then_inc(y_loaded, 16)
                    sp.wait_ge(z2_set[TT - 1], sp.snap(b + 2))
                    sp.dma_start(y_res[:].rearrange("p t d -> p (t d)"), x1_dram[b + 1]).then_inc(y_res_loaded, 16)
                sp.wait_ge(x1_set, sp.snap(b + BATCH + 1))
                sp.dma_start(out[b], x1[:]).then_inc(stored, 16)

            with sp.Fori(0, BATCH - 1) as b:
                ff_batch(b, True)
            ff_batch(BATCH - 1, False)
            sp.wait_ge(stored, 16 * BATCH + 16)

        @block.tensor
        def _(pe):
            pe.wait_ge(w_loaded, 16 * 14)
            for h in range(HEADS):
                mm = pe.matmul(bank[h // 8][:, (h % 8) * 64:(h % 8) * 64 + 64], wqn[:, h], wkn[:, h],
                               start=True, stop=True)
            mm.then_inc(m_made, 1)
            for h in range(HEADS):
                r = 64 if h % 2 == 0 else 0
                mm = pe.matmul(bank[2][r:r + 64, h:h + 1], wkn[:, h], b_qn[:, h:h + 1], start=True, stop=True)
            mm.then_inc(m_made, 1)
            for h in range(HEADS):
                a = h // 2
                r = 64 * (h % 2)
                mm = pe.matmul(bank[3 + a // 2][r:r + 64, (a % 2) * DIM:(a % 2) * DIM + DIM], wv[:, h], wo[:, h],
                               start=True, stop=True)
            mm.then_inc(g_made, 1)
            pe.wait_ge(bv_wide_set, 1)
            for h in range(HEADS):
                mm = pe.matmul(bank[7][:, 0:DIM], bv_wide[:, h], wo[:, h], start=(h == 0), stop=(h == HEADS - 1))
            mm.then_inc(g_made, 1)
            pe.wait_ge(wq_full, 1)
            pe.wait_ge(attn_w_set, 3)

            def latent(c, b):
                if c == 0:
                    pe.wait_ge(xt_loaded, pe.snap(16 * b + 16))
                if c == 3:
                    pe.wait_ge(cq_raw_set, pe.snap(b + 1))
                for d in range(DC):
                    mm = pe.matmul(q_bank[c % 3][:], w_a[:, d, c], x_t[:, d], start=(d == 0), stop=(d == DC - 1))
                mm.then_inc(proj[c], 1)

            def between(b):
                pe.wait_ge(q_cos, pe.snap(b * PAIRS + 1))
                for k in range(TT):
                    for d in range(DC):
                        mm = pe.matmul(q_bank[2][:, k * RANK:(k + 1) * RANK], x_t[:, d, k * P:(k + 1) * P],
                                       w_a[:, d, 1, ROPE:P], start=(d == 0), stop=(d == DC - 1))
                mm.then_inc(proj[4], 1)

            def step(T, S, Q, latents=False, values=False):
                def values_of(kt):
                    pe.wait_ge(pt_set[kt], T.n1)
                    pe.wait_ge(pt_set[TT + kt], T.n1 if kt < 2 else T.n2)
                    if kt == 0:
                        pe.wait_ge(v_set, T.b1)
                        pe.wait_ge(u_set, T.n1)
                    for h2 in range(2):
                        mm = pe.matmul(u_bank[64 * h2:64 * h2 + 64, :], v_lat[:, kt], probs_t[:, h2 * TT + kt],
                                       start=(kt == 0), stop=(kt == TT - 1))
                    mm.then_inc(pv[kt], 1)

                for j in range(TILES):
                    h, qt = divmod(j, TT)
                    if T is not None:
                        kt = j % TT
                        if kt == 0:
                            pe.wait_ge(probs_set[h], T.n1)
                        if j >= 2:
                            pe.wait_ge(pt_set[j - 2], T.n1)
                        else:
                            pe.wait_ge(pt_set[6 + j], T.n1)
                        for q in range(TT):
                            mm = pe.transpose(pt_bank[j % 2][:, q * P:(q + 1) * P],
                                              probs[:, T.buf, h * TT + q, kt * P:(kt + 1) * P], ident[:])
                        mm.then_inc(turned[j], 1)
                    if S is not None:
                        if j == 0:
                            pe.wait_ge(q_hi0_set, S.n1)
                            pe.wait_ge(q_lo0_set, S.n1)
                            pe.wait_ge(k_hi_set, S.b1)
                            pe.wait_ge(k_lo_set, S.b1)
                        if j == TT:
                            pe.wait_ge(q_hi_set, S.n1)
                            pe.wait_ge(q_lo_set, S.n1)
                        pe.wait_ge(exp_done[(j - 2) % TILES], S.n1)
                        cols = slice(qt * P, (qt + 1) * P)
                        pe.matmul(s_bank[j % 2][:], q_hi[:, S.buf, h, cols], k_hi[:, h], start=True, stop=False)
                        pe.matmul(s_bank[j % 2][:], q_hi[:, S.buf, h, cols], k_lo[:, h], start=False, stop=False)
                        pe.matmul(s_bank[j % 2][:], q_lo[:, S.buf, h, cols], k_hi[:, h], start=False,
                                  stop=True).then_inc(scores[j], 1)
                    if latents and j < 4:
                        latent(j, Q.b0)
                    if Q is not None:
                        for c in {0: [0], 1: [1], 2: [2]}.get(j, []) if not latents else {5: [0, 1], 6: [2]}.get(j, []):
                            if c == 0:
                                pe.wait_ge(staged[Q.buf], pe.snap((Q.b0 * PAIRS + Q.pair) * 8 + (8 if Q.buf else 16)))
                            if c == 0 and latents:
                                pe.wait_ge(cq_set, Q.b1)
                                pe.wait_ge(k_read, pe.snap(3 * Q.b0 + 3))
                            if c == 2 and values:
                                pe.wait_ge(v_next_set, Q.b1)
                            for s in range(2):
                                mm = pe.matmul(q_bank[c][:], wq_stage[:, Q.buf, s, c * P:(c + 1) * P], cq[:],
                                               start=(s == 0), stop=(s == 1))
                            mm.then_inc(qproj[c], 1)
                    if T is not None and j > TT:
                        values_of(kt=j - TT - 1)
                if T is not None:
                    values_of(kt=TT - 1)

            def turn(b, later):
                pe.wait_ge(y_loaded, pe.snap(16 * b + 16))
                if later:
                    for m in range(2):
                        pe.wait_ge(half_set[m], pe.snap(b * (UNITS // 2)))
                for d in range(DC):
                    for q in range(TT):
                        mm = pe.transpose(bank[d][:, q * P:(q + 1) * P], y_tok[:, q, d * P:(d + 1) * P], ident[:])
                mm.then_inc(y_turned, 1)

            def route(b, later):
                pe.wait_ge(y_raw_set, pe.snap(b + 1))
                if later:
                    pe.wait_ge(gated[0], pe.snap(b * (ROUTED // 2)))
                for q in range(TT):
                    for d in range(DC):
                        mm = pe.matmul(bank[2][:, q * EXPERTS:(q + 1) * EXPERTS], y_raw[:, d, q * P:(q + 1) * P],
                                       w_g[:, d], start=(d == 0), stop=(d == DC - 1))
                mm.then_inc(routed, 1)

            def finish(b, more):
                def project(q, pairs):
                    cols = slice(q * P, (q + 1) * P)
                    for a in pairs:
                        dst = q_bank[q % 3][:, 0:DIM]
                        pe.matmul(dst, u_hi[:, a, cols], g_hi[:, a], start=(a == 0), stop=False)
                        pe.matmul(dst, u_hi[:, a, cols], g_lo[:, a], start=False, stop=False)
                        mm = pe.matmul(dst, u_lo[:, a, cols], g_hi[:, a], start=False, stop=(a == PAIRS - 1))
                    if a == PAIRS - 1:
                        mm.then_inc(oproj[q], 1)
                pe.wait_ge(u_set, pe.snap(b * PAIRS + PAIRS))
                if more:
                    pe.wait_ge(q_cos, pe.snap(b * PAIRS + PAIRS + 2))
                for q in range(3):
                    project(q, range(PAIRS - 1))
                if not more:
                    turn(0, False)
                pe.wait_ge(u_set, pe.snap(b * PAIRS + PAIRS + 1))
                for q in range(3):
                    project(q, [PAIRS - 1])
                pe.wait_ge(z_set[0], pe.snap(b + 2))
                project(3, range(PAIRS))
                if not more:
                    pe.wait_ge(small_loaded, 16 * 6)
                    route(0, False)
                if more:
                    for q in range(1, TT):
                        pe.wait_ge(z_set[q], pe.snap(b + 2))

            walk(pe, step, between, finish)

            def product(dst, w, unit):
                for d in range(DC):
                    pe.matmul(dst, w[:, 0, d, unit], y_hi[:, d], start=(d == 0), stop=False)
                    pe.matmul(dst, w[:, 1, d, unit], y_hi[:, d], start=False, stop=False)
                    mm = pe.matmul(dst, w[:, 0, d, unit], y_lo[:, d], start=False, stop=(d == DC - 1))
                return mm

            def ff_batch(b, more):
                b1 = pe.snap(b + 1)
                b2 = pe.snap(b + 2)
                at = [pe.snap(b * (UNITS // 2) + k) for k in range(UNITS // 2 + 2)]
                at_e = [pe.snap(b * (ROUTED // 2) + k) for k in range(ROUTED // 2 + 1)]
                pe.wait_ge(y_hi_set, b1)
                pe.wait_ge(y_lo_set, b1)
                for u in range(UNITS):
                    if u >= 2:
                        pe.wait_ge(half_set[u % 2], at[u // 2])
                    if u >= SHARED + 2:
                        pe.wait_ge(gated[u % 2], at_e[u // 2 - 1])
                    if u < SHARED:
                        product(bank[u % 2][:], w_sh_v, u).then_inc(pre[u % 2], 1)
                    else:
                        product(bank[u % 2][:], w_in_v, u - SHARED)
                        if u == SHARED:
                            pe.wait_ge(route_step, pe.snap(ROUTE_STEPS * b + 1))
                        product(bank[2 + u % 2][:], w_in_v, ROUTED + u - SHARED).then_inc(pre[u % 2], 1)
                    if u == 1:
                        pe.wait_ge(route_step, pe.snap(ROUTE_STEPS * b + ROUTE_STEPS))
                        pe.wait_ge(z2_set[3], b1)
                        for q in range(TT):
                            mm = pe.transpose(bank[7][0:EXPERTS, q * P:(q + 1) * P], w_tok[:, q], ident[:])
                        mm.then_inc(w_turned, 1)
                    if u >= SHARED:
                        if u == SHARED + 1:
                            pe.wait_ge(fw_hi_set, 3)
                            pe.wait_ge(w_hi_set, b1)
                            pe.wait_ge(w_lo_set, b1)
                        if u >= SHARED + 2:
                            pe.wait_ge(h_set[u % 2], at[u // 2])
                        for e in {SHARED: [], SHARED + 1: [0, 1]}.get(u, [u - SHARED]):
                            for s in range(2):
                                mm = pe.matmul(bank[4 + e % 2][:], sel[:, e], w_t_split[:, s],
                                               start=(s == 0), stop=(s == 1))
                            mm.then_inc(widened[e % 2], 1)
                if more:
                    nb = pe.snap(b + 1)
                    turn(nb, True)
                pe.wait_ge(fw_hi_set, 4)
                pe.wait_ge(out_lo_set, 1)

                def project(q, units):
                    dst = bank[6 + q % 2][:, 0:DIM]
                    cols = slice(q * P, (q + 1) * P)
                    for u in units:
                        if u == 0:
                            pe.wait_ge(z2_set[(q - 2) % TT], b2 if q >= 2 else b1)
                            pe.matmul(dst, w_t[:, cols], b_down[:], start=True, stop=False)
                        if q == 0:
                            pe.wait_ge(h_hi_set[u % 2], at[u // 2 + 1])
                            pe.wait_ge(h_lo_set[u % 2], at[u // 2 + 2])
                        pe.matmul(dst, h_hi[:, u, cols], w_out_hi[:, u], start=False, stop=False)
                        pe.matmul(dst, h_hi[:, u, cols], w_out_lo[:, u], start=False, stop=False)
                        mm = pe.matmul(dst, h_lo[:, u, cols], w_out_hi[:, u], start=False, stop=(u == UNITS - 1))
                    if u == UNITS - 1:
                        mm.then_inc(down[q], 1)
                for q in range(2):
                    project(q, range(UNITS - 1))
                for q in range(2):
                    project(q, [UNITS - 1])
                if more:
                    route(nb, True)
                for q in range(2, TT):
                    project(q, range(UNITS))

            pe.wait_ge(fw_hi_set, 2)
            pe.wait_ge(fw_lo_set, 2)
            for i in range(TT):
                pe.wait_ge(z_set[i], BATCH + 1)
            with pe.Fori(0, BATCH - 1) as b:
                ff_batch(b, True)
            ff_batch(BATCH - 1, False)

        @block.scalar
        def _(act):
            act.wait_ge(m_made, 1)
            act.wait_ge(w_loaded, 16 * 14)
            for k in range(2):
                m4 = bank[k][:].rearrange("p (a s j) -> p a s j", s=2, j=64)
                act.copy(wq_raw[:, 4 * k:4 * k + 4, 0, 64:128], m4[:, :, 0, :])
                last = act.copy(wq_raw[:, 4 * k:4 * k + 4, 1, 0:64], m4[:, :, 1, :])
            last.then_inc(wq_full, 1)
            act.wait_ge(wq_full, 1)
            act.copy(wq_split[:, :, 0, :], wq_raw.rearrange("p a c m -> p a (c m)")).then_inc(wq_hi_set, 1)
            act.wait_ge(g_made, 1)
            for k in range(4):
                act.copy(g_hi[:, 2 * k:2 * k + 2, :], bank[3 + k][:].rearrange("p (a n) -> p a n", a=2))\
                   .then_inc(g_hi_set, 1)

            def step(T, S, Q, latents=False, values=False):
                def exp(j):
                    act.wait_ge(rowmax[j], S.n1)
                    act.activation(probs[:, S.buf, j], s_bank[j % 2][:], ACT.Exp,
                                   bias=neg_max[:, S.buf, j:j + 1],
                                   accum_out=sums[:, S.buf, j:j + 1]).then_inc(exp_done[j], 1)

                def q_high(c):
                    act.wait_ge(q_added if c else q_added0, Q.n1)
                    act.copy(q_hi[:, Q.buf, c], roped[:, c]).then_inc(q_hi_set if c else q_hi0_set, 1)
                for j in range(TILES):
                    if T is not None:
                        act.wait_ge(turned[j], T.n1)
                        act.wait_ge(pv[j % TT], T.n1)
                        act.copy(probs_t[:, j], pt_bank[j % 2][:]).then_inc(pt_set[j], 1)
                    if S is not None and j >= 1:
                        exp(j - 1)
                    if latents and j == 1:
                        act.wait_ge(proj[0], Q.b1)
                        act.activation(cq_raw[:], q_bank[0][:], ACT.Identity, bias=b_a[:, 0:1])\
                            .then_inc(cq_raw_set, 1)
                        act.wait_ge(cq_raw_set, Q.b1)
                        act.copy(cq[:], cq_raw[:]).then_inc(cq_hi_set, 1)
                    if Q is not None and not latents and j == 5:
                        q_high(0)
                    if Q is not None and not latents and j == 6:
                        q_high(1)
                if latents:
                    act.wait_ge(k_full, act.snap(2 * Q.b0 + 2))
                    if S is not None:
                        act.wait_ge(scores[TILES - 1], S.n1)
                    act.activation(k_hi[:], k_rope[:], ACT.Identity, scale=SCALE).then_inc(k_hi_set, 1)
                if S is not None:
                    exp(TILES - 1)
                if latents:
                    q_high(0)
                    q_high(1)
                if T is not None:
                    act.wait_ge(pv[TT - 1], T.n2)
                    act.copy(u_hi[:, T.pair], u_bank[:]).then_inc(u_hi_set, 1)
                if values:
                    act.wait_ge(v_next_set, Q.b1)
                    act.copy(v_lat[:], v_next[:]).then_inc(v_set, 1)

            walk(act, step, lambda b: None, lambda b, more: None)

            def take_rows(b):
                act.wait_ge(y_turned, act.snap(b + 1))
                act.copy(y_raw[:, 0], bank[0][:])
                act.copy(y_raw[:, 1], bank[1][:]).then_inc(y_raw_set, 1)
                act.wait_ge(y_raw_set, act.snap(b + 1))
                act.copy(y_hi[:], y_raw[:]).then_inc(y_hi_set, 1)
                act.wait_ge(route_step, act.snap(ROUTE_STEPS * b + ROUTE_EXP))
                act.activation(odds[:], shifted[:], ACT.Exp).then_inc(odds_set, 1)

            def ff_batch(b, more):
                b1 = act.snap(b + 1)
                at = [act.snap(b * (UNITS // 2) + k) for k in range(UNITS // 2 + 2)]
                at_e = [act.snap(b * (ROUTED // 2) + k) for k in range(ROUTED // 2 + 1)]

                def split_hi(u):
                    act.wait_ge(h_set[u % 2], at[u // 2 + 1])
                    act.copy(h_hi[:, u], hidden[:, u % 2]).then_inc(h_hi_set[u % 2], 1)

                for u in range(UNITS):
                    act.wait_ge(pre[u % 2], at[u // 2 + 1])
                    if u >= SHARED + 2:
                        act.wait_ge(silu_set[u % 2], at_e[u // 2 - 1])
                    act.activation(half_pre[:, u % 2], bank[u % 2][:], ACT.Identity, bias=b_pre[:, u:u + 1],
                                   scale=0.5).then_inc(half_set[u % 2], 1)
                    act.wait_ge(half_set[u % 2], at[u // 2 + 1])
                    act.activation(tanh_pre[:, u % 2], half_pre[:, u % 2], ACT.Tanh).then_inc(tanh_set[u % 2], 1)
                    if u == 1:
                        act.wait_ge(w_turned, b1)
                        act.copy(w_t, bank[7][0:EXPERTS, :]).then_inc(w_t_set, 1)
                        act.wait_ge(w_t_set, b1)
                        act.copy(w_t_split[:, 0], w_t).then_inc(w_hi_set, 1)
                    if u >= 1:
                        split_hi(u - 1)
                split_hi(UNITS - 1)
                if more:
                    take_rows(act.snap(b + 1))

            act.wait_ge(fw_loaded, 16 * 2)
            act.copy(wq_stage[:].rearrange(flat)[:, 0:n_sh], raw_sh).then_inc(fw_hi_set, 1)
            act.copy(wq_split[:].rearrange(flat)[:, 0:n_in], raw_in).then_inc(fw_hi_set, 1)
            take_rows(0)
            act.wait_ge(fw_late_loaded, 16 * 2)
            act.copy(sel, sel_raw).then_inc(fw_hi_set, 1)
            act.wait_ge(oproj[TT - 1], BATCH)
            act.copy(w_out_hi[:], raw_out).then_inc(fw_hi_set, 1)
            act.wait_ge(b_half_set, 1)
            with act.Fori(0, BATCH - 1) as b:
                ff_batch(b, True)
            ff_batch(BATCH - 1, False)

        @block.vector
        def _(dve):
            dve.memset(ones[:], 1.0).then_inc(consts_set, 1)
            dve.wait_ge(w_loaded, 16 * 14)
            dve.wait_ge(consts_set, 1)
            for h in range(HEADS):
                last = dve.tensor_scalar(bv_wide[:, h], ones[:], b_v[:, h:h + 1], None, ALU.mult)
            last.then_inc(bv_wide_set, 1)
            dve.wait_ge(m_made, 2)
            bm = bank[2][:, 0:HEADS].rearrange("p (a s) -> p a s", s=2)
            dve.tensor_copy(b_q[64:128, :, 0], bm[64:128, :, 0])
            dve.tensor_copy(b_q[0:64, :, 1], bm[0:64, :, 1]).then_inc(attn_w_set, 1)
            dve.wait_ge(wq_hi_set, 1)
            dve.tensor_tensor(wq_split[:, :, 1, :], wq_raw.rearrange("p a c m -> p a (c m)"),
                              wq_split[:, :, 0, :].bitcast(F32), ALU.subtract).then_inc(wq_lo_set, 1)
            for k in range(4):
                dve.wait_ge(g_hi_set, k + 1)
                last = dve.tensor_tensor(g_lo[:, 2 * k:2 * k + 2, :], bank[3 + k][:].rearrange("p (a n) -> p a n", a=2),
                                         g_hi[:, 2 * k:2 * k + 2, :].bitcast(F32), ALU.subtract)
            last.then_inc(attn_w_set, 1)
            dve.wait_ge(g_made, 2)
            dve.tensor_tensor(b_o[:], bank[7][:, 0:DIM], b_o[:], ALU.add).then_inc(attn_w_set, 1)
            dve.memset(minus_half[:], -0.5).then_inc(consts_set, 1)

            dve.memset(w_tok[:], 0.0).then_inc(fw_const, 1)
            dve.wait_ge(fw_const, 1)
            dve.memset(w_tok[:, :, ROUTED:ROUTED + 1], 1.0).then_inc(fw_const, 1)
            dve.wait_ge(fw_const, 2)
            dve.wait_ge(small_loaded, 16 * 6)
            dve.tensor_scalar(b_pre[:], b_pre[:], 0.5, None, ALU.mult).then_inc(b_half_set, 1)

            def normalise_rows(n, z_done, b2, free, free_value):
                for q in range(TT):
                    dve.wait_ge(z_done[q], b2)
                    if q >= 1:
                        dve.wait_ge(stats_set, dve.snap(TT * n + q))
                    dve.bn_stats(stats[:, q], z[:, q]).then_inc(stats_set, 1)
                    if q >= 1:
                        last = dve.bn_aggr(mv[:, q - 1], stats[:, q - 1])
                last.then_inc(mv_set, 1)
                dve.wait_ge(stats_set, dve.snap(TT * n + TT))
                dve.wait_ge(mv_set, dve.snap(2 * n + 1))
                dve.tensor_scalar(var_e[:, 0:TT - 1], mv[:, 0:TT - 1, 1], EPS, None, ALU.add)
                dve.bn_aggr(mv[:, TT - 1], stats[:, TT - 1]).then_inc(mv_set, 1)
                dve.wait_ge(mv_set, dve.snap(2 * n + 2))
                dve.tensor_scalar(var_e[:, TT - 1:], mv[:, TT - 1:, 1], EPS, None, ALU.add)\
                   .then_inc(var_set, 1)
                dve.wait_ge(rstd_set, dve.snap(n + 1))
                dve.wait_ge(free, free_value)
                for q in range(TT):
                    last = dve.tensor_scalar(x1[:, q], z[:, q], mv[:, q, 0:1], rstd[:, q:q + 1],
                                             ALU.subtract, ALU.mult)
                last.then_inc(x1_set, 1)

            def step(T, S, Q, latents=False, values=False):
                def normalise(j):
                    dve.wait_ge(exp_done[j], S.n1 if j < 6 else S.n2)
                    dve.reciprocal(inv[:, S.buf, j:j + 1], sums[:, S.buf, j:j + 1]).then_inc(inv_set[j], 1)
                    dve.wait_ge(inv_set[j], S.n1)
                    op = dve.tensor_scalar(probs[:, S.buf, j], probs[:, S.buf, j], inv[:, S.buf, j:j + 1],
                                           None, ALU.mult)
                    if j % TT == TT - 1:
                        op.then_inc(probs_set[j // TT], 1)

                def key(c):
                    dve.wait_ge(proj[c + 1], Q.b1)
                    dve.scalar_tensor_tensor(out=k_rope[:, c] if c < 2 else rot[:], in0=q_bank[(c + 1) % 3][:],
                                             scalar=b_a[:, c + 1:c + 2], in1=rope[:, c],
                                             op0=ALU.add, op1=ALU.mult).then_inc(k_read, 1)

                def query(c):
                    dve.wait_ge(qproj[c], Q.n1 if c < 2 else dve.snap(Q.b0 * PAIRS + Q.pair + 3))
                    if c == 1 and S is not None:
                        dve.wait_ge(q_lo_set, S.n1)
                    op = dve.scalar_tensor_tensor(out=roped[:, c] if c < 2 else rot[:], in0=q_bank[c][:],
                                                  scalar=b_q[:, Q.pair, c:c + 1], in1=rope[:, c],
                                                  op0=ALU.add, op1=ALU.mult)
                    if c == 2:
                        op.then_inc(q_cos, 1)
                for j in range(TILES):
                    if S is not None:
                        dve.wait_ge(scores[j], S.n1)
                        dve.tensor_reduce(neg_max[:, S.buf, j:j + 1], s_bank[j % 2][:], AX.X, ALU.max,
                                          negate=True).then_inc(rowmax[j], 1)
                        if j >= 1:
                            normalise(j - 1)
                    if latents:
                        if 2 <= j <= 4:
                            key(j - 2)
                        if j == 3:
                            dve.wait_ge(cq_hi_set, Q.b1)
                            dve.tensor_tensor(cq[64:128], cq_raw[64:128], cq[64:128].bitcast(F32), ALU.subtract)\
                               .then_inc(cq_set, 1)
                        if j == 5:
                            dve.wait_ge(k_read, dve.snap(3 * Q.b0 + 3))
                            dve.tensor_tensor(k_rope[0:64, 0], k_rope[0:64, 0], rot[0:64], ALU.add)\
                               .then_inc(k_full, 1)
                            dve.tensor_tensor(k_rope[64:128, 1], k_rope[64:128, 1], rot[64:128], ALU.add)\
                               .then_inc(k_full, 1)
                        if j == 6:
                            query(0)
                            query(1)
                        if j == 7:
                            dve.wait_ge(k_full, dve.snap(2 * Q.b0 + 2))
                            query(2)
                    elif Q is not None and 1 <= j <= 3:
                        query(j - 1)
                if latents:
                    dve.wait_ge(k_hi_set, Q.b1)
                    dve.scalar_tensor_tensor(out=k_lo[:], in0=k_rope[:], scalar=SCALE, in1=k_hi[:].bitcast(F32),
                                             op0=ALU.mult, op1=ALU.subtract).then_inc(k_lo_set, 1)
                if S is not None:
                    normalise(TILES - 1)
                if latents:
                    dve.wait_ge(proj[4], Q.b1)
                    dve.tensor_tensor(v_next[:], q_bank[2][:, 0:TT * RANK].rearrange("p (k r) -> p k r", k=TT),
                                      b_kv[:].rearrange("p (a r) -> p a r", a=1).to_broadcast([P, TT, RANK]),
                                      ALU.add).then_inc(v_next_set, 1)
                if T is not None:
                    dve.wait_ge(u_hi_set, T.n1)
                    dve.tensor_tensor(u_lo[:, T.pair], u_bank[:], u_hi[:, T.pair].bitcast(F32), ALU.subtract)\
                       .then_inc(u_set, 1)

            def low_rows(b):
                dve.wait_ge(y_hi_set, dve.snap(b + 1))
                dve.tensor_tensor(y_lo[:], y_raw[:], y_hi[:].bitcast(F32), ALU.subtract).then_inc(y_lo_set, 1)

            def route(b):
                steps = [0]

                def then(ins):
                    steps[0] += 1
                    ins.then_inc(route_step, 1)
                    dve.wait_ge(route_step, dve.snap(ROUTE_STEPS * b + steps[0]))
                dve.wait_ge(routed, dve.snap(b + 1))
                e3 = [P, TT, EXPERTS]
                then(dve.tensor_tensor(gate[:], bank[2][:, 0:TT * EXPERTS].rearrange("p (t e) -> p t e", t=TT),
                                       b_g[:].rearrange("p (a e) -> p a e", a=1).to_broadcast(e3), ALU.add))
                then(dve.tensor_reduce(top[:], gate[:], AX.X, ALU.max, negate=True))
                then(dve.tensor_tensor(shifted[:], gate[:],
                                       top[:].rearrange("p (t a) -> p t a", a=1).to_broadcast(e3), ALU.add))
                assert steps[0] == ROUTE_EXP
                other = gate[:].rearrange("p t (a f) -> p t a f", a=1).to_broadcast([P, TT, EXPERTS, EXPERTS])
                own = gate[:].rearrange("p t (e a) -> p t e a", a=1).to_broadcast([P, TT, EXPERTS, EXPERTS])
                then(dve.tensor_tensor(above, other, own, ALU.is_gt))
                then(dve.tensor_tensor(ties, other, own, ALU.is_equal))
                f3 = "p t e f -> p t (e f)"
                then(dve.tensor_tensor(ties.rearrange(f3), ties.rearrange(f3),
                                       before[:].rearrange("p (a e) -> p a e", a=1).to_broadcast([P, TT, 64]),
                                       ALU.mult))
                then(dve.tensor_tensor(above, above, ties, ALU.add))
                then(dve.tensor_reduce(rank[:], above, AX.X, ALU.add))
                then(dve.tensor_scalar(chosen[:], rank[:], float(ROUTED), None, ALU.is_lt))
                dve.wait_ge(odds_set, dve.snap(b + 1))
                then(dve.tensor_tensor(picked[:], odds[:], chosen[:], ALU.mult))
                then(dve.tensor_reduce(total[:], picked[:], AX.X, ALU.add))
                then(dve.reciprocal(inv_total[:], total[:]))
                then(dve.tensor_tensor(w_tok[:, :, 0:ROUTED], picked[:, :, 0:ROUTED],
                                       inv_total[:].rearrange("p (t a) -> p t a", a=1).to_broadcast([P, TT, ROUTED]),
                                       ALU.mult))
                assert steps[0] == ROUTE_STEPS

            def split_low():
                for n, (lo, raw, hi) in enumerate((
                        (wq_stage[:].rearrange(flat)[:, n_sh:2 * n_sh], raw_sh, wq_stage[:].rearrange(flat)[:, 0:n_sh]),
                        (wq_split[:].rearrange(flat)[:, n_in:2 * n_in], raw_in, wq_split[:].rearrange(flat)[:, 0:n_in]))):
                    dve.wait_ge(fw_hi_set, n + 1)
                    dve.tensor_tensor(lo, raw, hi.bitcast(F32), ALU.subtract).then_inc(fw_lo_set, 1)

            def finish(b, more):
                b1 = dve.snap(b + 1)
                if not more:
                    split_low()
                    low_rows(0)
                dve.wait_ge(xb_set, b1)
                for q in range(TT):
                    dve.wait_ge(oproj[q], b1)
                    dve.tensor_tensor(z[:, q], q_bank[q % 3][:, 0:DIM], x_b[:, q], ALU.add).then_inc(z_set[q], 1)
                if not more:
                    route(0)
                normalise_rows(b, z_set, dve.snap(b + 2), x1_stored, dve.snap(16 * b + 16))

            walk(dve, step, lambda b: None, finish)

            def ff_batch(b, more):
                b1 = dve.snap(b + 1)
                b2 = dve.snap(b + 2)
                at = [dve.snap(b * (UNITS // 2) + k) for k in range(UNITS // 2 + 2)]
                at_e = [dve.snap(b * (ROUTED // 2) + k) for k in range(ROUTED // 2 + 1)]
                for u in range(UNITS):
                    if u == SHARED:
                        dve.wait_ge(w_hi_set, b1)
                        dve.tensor_tensor(w_t_split[:, 1], w_t, w_t_split[:, 0].bitcast(F32), ALU.subtract)\
                           .then_inc(w_lo_set, 1)
                    dve.wait_ge(tanh_set[u % 2], at[u // 2 + 1])
                    if u >= 2:
                        dve.wait_ge(h_hi_set[u % 2], at[u // 2])
                    dve.wait_ge(h_lo_set[u % 2], at[u // 2 + 1])
                    op = dve.scalar_tensor_tensor(out=hidden[:, u % 2], in0=tanh_pre[:, u % 2], scalar=1.0,
                                                  in1=half_pre[:, u % 2], op0=ALU.add, op1=ALU.mult)
                    if u < SHARED:
                        op.then_inc(h_set[u % 2], 1)
                        continue
                    op.then_inc(silu_set[u % 2], 1)
                    dve.wait_ge(silu_set[u % 2], at_e[u // 2])
                    dve.scalar_tensor_tensor(out=hidden[:, u % 2], in0=bank[2 + u % 2][:], scalar=b_up[:, u:u + 1],
                                             in1=hidden[:, u % 2], op0=ALU.add, op1=ALU.mult).then_inc(gated[u % 2], 1)
                    dve.wait_ge(gated[u % 2], at_e[u // 2])
                    dve.wait_ge(widened[u % 2], at_e[u // 2])
                    dve.tensor_tensor(hidden[:, u % 2], bank[4 + u % 2][:], hidden[:, u % 2], ALU.mult)\
                       .then_inc(h_set[u % 2], 1)
                if more:
                    nb = dve.snap(b + 1)
                    low_rows(nb)
                dve.wait_ge(y_res_loaded, dve.snap(16 * b + 16))
                for q in range(TT):
                    if more and q == 2:
                        route(nb)
                    dve.wait_ge(down[q], b1)
                    dve.tensor_tensor(z[:, q], bank[6 + q % 2][:, 0:DIM], y_res[:, q], ALU.add).then_inc(z2_set[q], 1)
                normalise_rows(b + BATCH, z2_set, b2, stored, dve.snap(16 * b + 16))

            with dve.Fori(0, BATCH - 1) as b:
                ff_batch(b, True)
            ff_batch(BATCH - 1, False)

        @block.gpsimd
        def _(pool):
            for s, n in [(z, 1) for z in z_set] + [(qproj[2], 2)] + [(s, 1) for s in exp_done[6:] + pt_set[6:] + pv]\
                    + [(u_set, 1)] + [(s, 1) for s in z2_set + h_lo_set] + [(stored, 16), (x1_stored, 16)]:
                pool.sem_inc(s, n)
            pool.wait_ge(attn_w_set, 3)
            pool.wait_ge(consts_set, 2)
            def step(T, S, Q, latents=False, values=False):
                if Q is None:
                    return
                pool.wait_ge(q_cos, Q.n1)
                pool.tensor_tensor(roped[0:64, 0], roped[0:64, 0], rot[0:64], ALU.add).then_inc(q_added0, 1)
                pool.wait_ge(q_added0, Q.n1)
                pool.tensor_tensor(roped[64:128, 1], roped[64:128, 1], rot[64:128], ALU.add).then_inc(q_added, 1)
                pool.wait_ge(q_added, Q.n1)
                pool.wait_ge(q_hi0_set, Q.n1)
                pool.tensor_tensor(q_lo[:, Q.buf, 0], roped[:, 0], q_hi[:, Q.buf, 0].bitcast(F32), ALU.subtract)\
                    .then_inc(q_lo0_set, 1)
                pool.wait_ge(q_hi_set, Q.n1)
                pool.tensor_tensor(q_lo[:, Q.buf, 1], roped[:, 1], q_hi[:, Q.buf, 1].bitcast(F32), ALU.subtract)\
                    .then_inc(q_lo_set, 1)

            def finish(b, more):
                pool.wait_ge(x_loaded, pool.snap(16 * b + 16))
                for i in range(TT):
                    last = pool.tensor_tensor(x_b[:, i], x_tok[:, i], b_o[:], ALU.add)
                last.then_inc(xb_set, 1)
                pool.wait_ge(var_set, pool.snap(b + 1))
                pool.tensor_tensor(rstd[:], var_e[:], minus_half[:], ALU.pow).then_inc(rstd_set, 1)

            walk(pool, step, lambda b: None, finish)

            pool.wait_ge(fw_hi_set, 4)
            pool.tensor_tensor(w_out_lo[:], raw_out, w_out_hi[:].bitcast(F32), ALU.subtract).then_inc(out_lo_set, 1)
            with pool.Fori(0, BATCH) as b:
                b1 = pool.snap(b + 1)
                at = [pool.snap(b * (UNITS // 2) + k) for k in range(UNITS // 2 + 2)]
                for u in range(UNITS):
                    pool.wait_ge(h_hi_set[u % 2], at[u // 2 + 1])
                    pool.tensor_tensor(h_lo[:, u], hidden[:, u % 2], h_hi[:, u].bitcast(F32), ALU.subtract)\
                        .then_inc(h_lo_set[u % 2], 1)
                pool.wait_ge(var_set, pool.snap(b + BATCH + 1))
                pool.tensor_tensor(rstd[:], var_e[:], minus_half[:], ALU.pow).then_inc(rstd_set, 1)


def layouts(inputs):
    g = {k.replace("L0_", ""): np.asarray(v) for k, v in inputs.items()}
    even, odd = np.arange(0, ROPE, 2), np.arange(1, ROPE, 2)
    pe, rt = np.concatenate([even, odd]), np.concatenate([odd, even])
    cat = np.concatenate
    x = g["attn_x"]
    o = {}
    o["x"] = x.reshape(BATCH, TT, P, DIM).transpose(0, 2, 1, 3)
    o["xT"] = x.reshape(BATCH * SEQ, DC, P).transpose(2, 1, 0)
    wqa, wkva = g["attn_wq_a_w"], g["attn_wkv_a_w"]
    kv, kpe, krt = wkva[:, :RANK], wkva[:, RANK + pe], wkva[:, RANK + rt]
    w_a = np.stack([cat([wqa, wqa], 1), cat([kpe, kv], 1), cat([kv, kpe], 1), cat([krt, krt], 1)], 1)
    o["w_a"] = w_a.reshape(DC, P, 4, P).transpose(1, 0, 2, 3)
    bqa, bkva = g["attn_wq_a_b"], g["attn_wkv_a_b"]
    bkv, bpe, brt = bkva[:RANK], bkva[RANK + pe], bkva[RANK + rt]
    o["b_a"] = np.stack([cat([bqa, bqa]), cat([bpe, bkv]), cat([bkv, bpe]), cat([brt, brt])], 1)
    o["b_kv"] = bkv[None]
    wqb = g["attn_wq_b_w"].reshape(RANK, HEADS, NOPE + ROPE)
    bqb = g["attn_wq_b_b"].reshape(HEADS, NOPE + ROPE)
    wkvb = g["attn_wkv_b_w"].reshape(RANK, HEADS, NOPE + VHD)
    bkvb = g["attn_wkv_b_b"].reshape(HEADS, NOPE + VHD)
    qn = wqb[:, :, :NOPE].transpose(2, 1, 0)
    o["wqn"] = cat([qn, qn], 2)
    o["wkn"] = wkvb[:, :, :NOPE].transpose(2, 1, 0)
    o["wv"] = wkvb[:, :, NOPE:].transpose(2, 1, 0)
    o["wo"] = g["attn_wo_w"].reshape(HEADS, VHD, DIM).transpose(1, 0, 2)
    o["b_qn"] = bqb[:, :NOPE].T
    o["b_v"] = bkvb[:, NOPE:].T
    o["b_o"] = g["attn_wo_b"][None]
    raw = np.zeros((P, PAIRS, 3, P), np.float32)
    b_q = np.zeros((P, PAIRS, 4), np.float32)
    for r in (slice(0, 64), slice(64, 128)):
        raw[r, :, 0, 0:64] = wqb[:, 0::2, NOPE + pe]
        raw[r, :, 1, 64:128] = wqb[:, 1::2, NOPE + pe]
        raw[r, :, 2, 0:64] = wqb[:, 0::2, NOPE + rt]
        raw[r, :, 2, 64:128] = wqb[:, 1::2, NOPE + rt]
    b_q[0:64, :, 0] = bqb[0::2, NOPE + pe].T
    b_q[64:128, :, 1] = bqb[1::2, NOPE + pe].T
    b_q[0:64, :, 2] = bqb[0::2, NOPE + rt].T
    b_q[64:128, :, 2] = bqb[1::2, NOPE + rt].T
    o["wq_raw"], o["b_q"] = raw, b_q
    def cols(w):
        return w.reshape(-1, DC, P, HID).transpose(2, 1, 0, 3)
    ws = g["ffn_Ws_up"].reshape(DIM, SHARED, HID).transpose(1, 0, 2)
    o["w_in"] = cols(cat([g["ffn_Wgate"], g["ffn_Wup"]], 0)).reshape(P, -1)
    o["w_sh"] = cols(ws).reshape(P, -1)
    o["w_out"] = cat([g["ffn_Ws_down"].reshape(SHARED, HID, DIM), g["ffn_Wdown"]], 0).transpose(1, 0, 2)
    o["w_g"] = g["ffn_Wg"].reshape(DC, P, EXPERTS).transpose(1, 0, 2)
    o["b_g"] = g["ffn_bg"][None]
    o["b_pre"] = cat([g["ffn_bs_up"].reshape(SHARED, HID), g["ffn_bgate"]], 0).T
    o["b_up"] = cat([np.zeros((SHARED, HID), np.float32), g["ffn_bup"]], 0).T
    o["b_down"] = cat([g["ffn_bdown"], g["ffn_bs_down"][None], np.zeros((1, DIM), np.float32)], 0)
    sel = np.zeros((EXPERTS, ROUTED, P), np.float32)
    for u in range(ROUTED):
        sel[u, u] = 1
    o["sel"] = sel
    o["before"] = np.tril(np.ones((EXPERTS, EXPERTS), np.float32), -1).reshape(1, -1)
    f = np.float32
    inv_freq = (f(1.0) / np.power(f(THETA), np.arange(0, ROPE, 2, dtype=f) / f(ROPE))).astype(f)
    ang = np.outer(np.arange(SEQ, dtype=f), inv_freq).astype(f)
    c, s = np.cos(ang).T.astype(f), np.sin(ang).T.astype(f)
    cc, ss, one = cat([c, c]), cat([-s, s]), np.ones((64, SEQ), f)
    o["rope"] = np.stack([cat([cc, one]), cat([one, cc]), cat([ss, ss])], 1)
    o["ident"] = np.eye(P, dtype=f)
    return {k: np.ascontiguousarray(v) for k, v in o.items()}


def kernel(**inputs):
    import concourse.bacc as bacc
    from concourse.bass_utils import run_bass_kernel_spmd

    nc = bacc.Bacc("TRN2", target_bir_lowering=False, num_devices=1)
    arrays, t = {}, {}
    for name, a in layouts(inputs).items():
        arrays[f"in_{name}"] = a
        t[name] = nc.dram_tensor(f"in_{name}", a.shape, mybir.dt.from_np(a.dtype), kind="ExternalInput").ap()
    out = nc.dram_tensor("out", (BATCH, SEQ, DIM), F32, kind="ExternalOutput").ap()
    program(nc, t, out.rearrange("b (t p) d -> b p t d", p=P))
    r = run_bass_kernel_spmd(nc, [arrays], core_ids=[0])
    return np.asarray(r.results[0]["out"])
```

```python
from contextlib import ExitStack

import numpy as np
import concourse.bass as bass
from concourse import mybir

F32 = mybir.dt.float32
F32R = mybir.dt.float32r
ALU = mybir.AluOpType
ACT = mybir.ActivationFunctionType
AX = mybir.AxisListType

P = 128
BATCH, SEQ, DIM = 8, 512, 256
HEADS, NOPE, ROPE, VHD = 16, 128, 64, 128
RANK = 64
PAIRS = HEADS // 2
DC = DIM // P
TT = SEQ // P
EXPERTS, ROUTED, HID = 8, 6, 128
SHARED = 2
UNITS = ROUTED + SHARED
EPS = 1e-5
THETA = 1000000.0
SCALE = 1.0 / float(np.sqrt(VHD))
TILES = 2 * TT
BLOCKS = [(0, 0), (0, 1), (1, 0), (1, 1), (0, 2), (1, 2), (0, 3), (1, 3)]
VALUES_AT = {3: 0, 4: 1, 6: 2, TILES: 3}
Q_AT = {0: [0], 1: [1], 2: [2]}
Q_AT_BEHIND_LATENTS = {4: [0, 1], 5: [2]}
ROUTE_STEPS, ROUTE_EXP = 13, 3


def program(nc, t, out):
    ctx = ExitStack()
    with ctx:
        def sb(name, shape, dt=F32):
            return ctx.enter_context(nc.sbuf_tensor(name, shape, dt))

        def sem(name):
            return ctx.enter_context(nc.semaphore(name))

        def sems(name, n):
            return [sem(f"{name}{i}") for i in range(n)]

        x1_dram = nc.dram_tensor("x1_scratch", (BATCH, P, TT * DIM), F32, kind="Internal").ap()

        bank = [ctx.enter_context(nc.psum_tensor(f"bank{i}", [P, 512], F32)) for i in range(8)]
        s_bank, pt_bank, q_bank, u_bank = bank[0:2], bank[2:4], bank[4:7], bank[7]

        arena = sb("arena", [P, 13312])

        def view(at, n):
            return arena[:, at:at + n]
        wq_raw = view(0, 3072).rearrange("p (a c m) -> p a c m", a=PAIRS, c=3)
        wqn = view(3072, 2048).rearrange("p (h i) -> p h i", h=HEADS)
        wkn = view(5120, 1024).rearrange("p (h j) -> p h j", h=HEADS)
        wv = view(6144, 1024).rearrange("p (h j) -> p h j", h=HEADS)
        wo = view(7168, 4096).rearrange("p (h n) -> p h n", h=HEADS)
        bv_wide = view(11264, 2048).rearrange("p (h m) -> p h m", h=HEADS)
        probs = view(0, 8192).rearrange("p (m j k) -> p m j k", m=2, j=TILES)
        probs_t = view(8192, 4096).rearrange("p (k q) -> p k q", k=TILES)

        ident = sb("ident", [P, P])
        rope = sb("rope", [P, 3, SEQ])
        w_a = sb("w_a", [P, DC, 4, P])
        b_a = sb("b_a", [P, 4])
        b_kv = sb("b_kv", [P, RANK])
        b_qn = sb("b_qn", [P, HEADS])
        b_v = sb("b_v", [P, HEADS])
        b_o = sb("b_o", [P, DIM])
        b_q = sb("b_q", [P, PAIRS, 4])
        ones = sb("ones", [P, P])
        wq_split = sb("wq_split", [P, PAIRS, 2, 3 * P], F32R)
        wq_stage = sb("wq_stage", [P, 2, 2, 3 * P], F32R)
        g_hi = sb("g_hi", [P, PAIRS, DIM], F32R)
        g_lo = sb("g_lo", [P, PAIRS, DIM], F32R)
        x_t = sb("x_t", [P, DC, SEQ])
        x_tok = sb("x_tok", [P, TT, DIM])
        x_b = sb("x_b", [P, TT, DIM])
        z = sb("z", [P, TT, DIM])
        x1 = sb("x1", [P, TT, DIM])
        stats = sb("stats", [P, TT, 6])
        mv = sb("mv", [P, TT, 2])
        var_e = sb("var_e", [P, TT])
        rstd = sb("rstd", [P, TT])
        minus_half = sb("minus_half", [P, TT])
        cq_raw = sb("cq_raw", [P, SEQ])
        cq = sb("cq", [P, SEQ], F32R)
        k_hi = sb("k_hi", [P, 2, SEQ], F32R)
        k_lo = sb("k_lo", [P, 2, SEQ], F32R)
        v_lat = sb("v_lat", [P, TT, RANK])
        k_rope = sb("k_rope", [P, 2, SEQ])
        v_next = sb("v_next", [P, TT, RANK])
        roped = sb("roped", [P, 2, SEQ])
        rot = sb("rot", [P, SEQ])
        q_hi = sb("q_hi", [P, 2, 2, SEQ], F32R)
        q_lo = sb("q_lo", [P, 2, 2, SEQ], F32R)
        neg_max = sb("neg_max", [P, 2, TILES])
        sums = sb("sums", [P, 2, TILES])
        inv = sb("inv", [P, 2, TILES])
        u_hi = sb("u_hi", [P, PAIRS, SEQ], F32R)
        u_lo = sb("u_lo", [P, PAIRS, SEQ], F32R)

        flat = "p a c m -> p (a c m)"
        n_in, n_sh = DC * 2 * ROUTED * HID, DC * SHARED * HID
        w_in_v = wq_split[:].rearrange("p a c m -> p (a c m)").rearrange(
            "p (s d u m) -> p s d u m", s=2, d=DC, u=2 * ROUTED)
        w_sh_v = wq_stage[:].rearrange("p a c m -> p (a c m)")[:, 0:2 * DC * SHARED * HID].rearrange(
            "p (s d u m) -> p s d u m", s=2, d=DC, u=SHARED)
        w_out_hi, w_out_lo = g_hi, g_lo
        h_hi, h_lo = u_hi, u_lo
        y_raw, y_hi, y_lo = roped, k_hi, k_lo
        y_tok, y_res = x_tok, x_b
        sel = q_hi[0:EXPERTS].rearrange("p a c m -> p (a c m)")[:, 0:ROUTED * P].rearrange(
            "p (u m) -> p u m", u=ROUTED)
        w_t_split = q_lo[0:EXPERTS, 0]
        raw_in = view(0, DC * 2 * ROUTED * HID)
        raw_sh = view(3072, DC * SHARED * HID)
        raw_out = view(4096, UNITS * DIM).rearrange("p (u n) -> p u n", u=UNITS)
        half_pre = view(6144, 2 * SEQ).rearrange("p (m q) -> p m q", m=2)
        tanh_pre = view(7168, 2 * SEQ).rearrange("p (m q) -> p m q", m=2)
        hidden = view(8192, 2 * SEQ).rearrange("p (m q) -> p m q", m=2)
        w_g = sb("w_g", [P, DC, EXPERTS])
        b_g = sb("b_g", [P, EXPERTS])
        b_pre = sb("b_pre", [P, UNITS])
        b_up = sb("b_up", [P, UNITS])
        b_down = sb("b_down", [EXPERTS, DIM])
        sel_raw = view(9216, ROUTED * P)[0:EXPERTS].rearrange("p (u m) -> p u m", u=ROUTED)
        before = sb("before", [P, EXPERTS * EXPERTS])
        gate = sb("gate", [P, TT, EXPERTS])
        above = view(9984, 256).rearrange("p (t e f) -> p t e f", t=TT, e=EXPERTS)
        ties = view(10240, 256).rearrange("p (t e f) -> p t e f", t=TT, e=EXPERTS)
        rank = sb("rank", [P, TT, EXPERTS])
        chosen = sb("chosen", [P, TT, EXPERTS])
        top = sb("top", [P, TT])
        shifted = sb("shifted", [P, TT, EXPERTS])
        odds = sb("odds", [P, TT, EXPERTS])
        picked = sb("picked", [P, TT, EXPERTS])
        total = sb("total", [P, TT])
        inv_total = sb("inv_total", [P, TT])
        w_tok = sb("w_tok", [P, TT, EXPERTS])
        w_t = view(10496, SEQ)[0:EXPERTS]

        m_loaded, q_loaded, k_loaded, g_loaded = sem("m_loaded"), sem("q_loaded"), sem("k_loaded"), sem("g_loaded")
        consts_set = sem("consts_set")
        m_made = sem("m_made")
        g_made = sem("g_made")
        wq_full = sem("wq_full")
        wq_hi_set = sem("wq_hi_set")
        wq_lo_set = sem("wq_lo_set")
        g_hi_set = sem("g_hi_set")
        attn_w_set = sem("attn_w_set")
        xt_loaded, x_loaded = sem("xt_loaded"), sem("x_loaded")
        proj = sems("proj", 5)
        cq_raw_set, cq_hi_set, cq_set = sem("cq_raw_set"), sem("cq_hi_set"), sem("cq_set")
        k_read, k_full, k_hi_set, k_lo_set = sem("k_read"), sem("k_full"), sem("k_hi_set"), sem("k_lo_set")
        v_next_set, v_set = sem("v_next_set"), sem("v_set")
        xb_set = sem("xb_set")
        oproj = sems("oproj", TT)
        z_set = sems("z_set", TT)
        stats_set, mv_set, var_set, rstd_set, x1_set = (
            sem("stats_set"), sem("mv_set"), sem("var_set"), sem("rstd_set"), sem("x1_set"))
        x1_stored = sem("x1_stored")
        staged = sems("staged", 2)
        qproj = sems("qproj", 3)
        q_cos = sem("q_cos")
        q_added0, q_added, q_hi_set, q_lo_set = sem("q_added0"), sem("q_added"), sem("q_hi_set"), sem("q_lo_set")
        q_hi0_set, q_lo0_set = sem("q_hi0_set"), sem("q_lo0_set")
        scores = sems("scores", TILES)
        rowmax = sems("rowmax", TILES)
        exp_done = sems("exp_done", TILES)
        inv_set = sems("inv_set", TILES)
        probs_set = sems("probs_set", 2)
        turned = sems("turned", TILES)
        pt_set = sems("pt_set", TILES)
        pv = sems("pv", TT)
        u_hi_set = sem("u_hi_set")
        u_set = sem("u_set")

        small_loaded = sem("small_loaded")
        fw_late_loaded, out_lo_set = sem("fw_late_loaded"), sem("out_lo_set")
        fw_loaded, fw_hi_set, fw_lo_set = sem("fw_loaded"), sem("fw_hi_set"), sem("fw_lo_set")
        y_loaded, y_turned, y_raw_set, y_hi_set, y_lo_set, y_res_loaded = (
            sem("y_loaded"), sem("y_turned"), sem("y_raw_set"), sem("y_hi_set"), sem("y_lo_set"), sem("y_res_loaded"))
        routed = sem("routed")
        route_step = sem("route_step")
        odds_set, w_turned, w_t_set, w_hi_set, w_lo_set = (
            sem("odds_set"), sem("w_turned"), sem("w_t_set"), sem("w_hi_set"), sem("w_lo_set"))
        pre = sems("pre", 2)
        half_set = sems("half_set", 2)
        tanh_set = sems("tanh_set", 2)
        silu_set = sems("silu_set", 2)
        gated = sems("gated", 2)
        widened = sems("widened", 2)
        h_set = sems("h_set", 2)
        h_hi_set = sems("h_hi_set", 2)
        h_lo_set = sems("h_lo_set", 2)
        down = sems("down", TT)
        z2_set = sems("z2_set", TT)
        stored = sem("stored")

        block = ctx.enter_context(nc.Block())

        class Item:
            def __init__(self, eng, b, pair, buf):
                self.pair, self.buf = pair, buf
                self.b1 = eng.snap(b + 1)
                self.b0 = b
                self.n1 = eng.snap(b * PAIRS + pair + 1)
                self.n2 = eng.snap(b * PAIRS + pair + 2)

        def walk(eng, step, between, finish, start=lambda: None):
            step(None, None, Item(eng, 0, 0, 0), latents=True)
            between(0)
            start()
            step(None, Item(eng, 0, 0, 0), Item(eng, 0, 1, 1), values=True)

            def batch(b, more):
                with eng.Fori(0, PAIRS // 2 - 1) as i:
                    a0, a1, a2, a3 = [Item(eng, b, 2 * i + k, k % 2) for k in range(4)]
                    step(a0, a1, a2)
                    step(a1, a2, a3)
                last = Item(eng, b, PAIRS - 1, 1)
                if more:
                    nb = eng.snap(b + 1)
                    first = Item(eng, nb, 0, 0)
                    step(Item(eng, b, PAIRS - 2, 0), last, first, latents=True)
                    between(nb)
                    step(last, first, Item(eng, nb, 1, 1), values=True)
                else:
                    step(Item(eng, b, PAIRS - 2, 0), last, None)
                    step(last, None, None)
                finish(b, more)

            with eng.Fori(0, BATCH - 1) as b:
                batch(b, True)
            batch(BATCH - 1, False)

        @block.sync
        def _(sp):
            for dst, src, loaded in ((wqn, t["wqn"], m_loaded), (wkn, t["wkn"], m_loaded), (b_qn[:], t["b_qn"], m_loaded),
                          (wq_raw, t["wq_raw"], q_loaded), (b_q[:], t["b_q"], q_loaded),
                          (w_a[:], t["w_a"], k_loaded), (x_t[:], t["xT"][:, :, 0:SEQ], xt_loaded),
                          (b_a[:], t["b_a"], k_loaded), (rope[:], t["rope"], k_loaded),
                          (b_kv[:], t["b_kv"].to_broadcast([P, RANK]), k_loaded),
                          (wv, t["wv"], g_loaded), (wo, t["wo"], g_loaded), (b_v[:], t["b_v"], g_loaded),
                          (b_o[:], t["b_o"].to_broadcast([P, DIM]), g_loaded),
                          (ident[:], t["ident"], g_loaded), (x_tok[:], t["x"][0], x_loaded)):
                sp.dma_start(dst, src).then_inc(loaded, 16)
            for dst, src in ((w_g[:], t["w_g"]), (b_g[:], t["b_g"].to_broadcast([P, EXPERTS])),
                             (b_pre[:], t["b_pre"]), (b_up[:], t["b_up"]), (b_down[:], t["b_down"]),
                             (before[:], t["before"].to_broadcast([P, EXPERTS * EXPERTS]))):
                sp.dma_start(dst, src).then_inc(small_loaded, 16)
            sp.wait_ge(wq_hi_set, 1)
            sp.wait_ge(wq_lo_set, 1)

            def stage(b, pair, m):
                sp.wait_ge(qproj[2], sp.snap(b * PAIRS + pair + 1))
                sp.dma_start(wq_stage[:, m].bitcast(F32), wq_split[:, pair].bitcast(F32)).then_inc(staged[m], 16)
            for pair in range(4):
                stage(0, pair, pair % 2)

            def batch(b, more):
                if more:
                    sp.wait_ge(proj[4], sp.snap(b + 1))
                    sp.dma_start(x_t[:], t["xT"][:, :, bass.ds((b + 1) * SEQ, SEQ)]).then_inc(xt_loaded, 16)
                with sp.Fori(2, PAIRS // 2) as i:
                    for m in range(2):
                        stage(b, 2 * i + m, m)
                if more:
                    for pair in range(4):
                        stage(b + 1, pair, pair % 2)
                    sp.wait_ge(xb_set, sp.snap(b + 1))
                    sp.dma_start(x_tok[:], t["x"][b + 1]).then_inc(x_loaded, 16)
                else:
                    sp.wait_ge(xb_set, BATCH)
                    sp.wait_ge(x1_stored, 32)
                    sp.dma_start(y_tok[:].rearrange("p t d -> p (t d)"), x1_dram[0]).then_inc(y_loaded, 16)
                    sp.wait_ge(turned[TILES - 1], BATCH * PAIRS - 1)
                    sp.dma_start(raw_sh, t["w_sh"]).then_inc(fw_loaded, 16)
                    sp.dma_start(raw_in, t["w_in"]).then_inc(fw_loaded, 16)
                    sp.wait_ge(turned[TILES - 1], BATCH * PAIRS)
                    sp.dma_start(raw_out, t["w_out"]).then_inc(fw_late_loaded, 16)
                    sp.wait_ge(pv[TT - 1], BATCH * PAIRS + 1)
                    sp.dma_start(sel_raw, t["sel"]).then_inc(fw_late_loaded, 16)
                    sp.wait_ge(z_set[TT - 1], BATCH + 1)
                    sp.dma_start(y_res[:].rearrange("p t d -> p (t d)"), x1_dram[0]).then_inc(y_res_loaded, 16)
                sp.wait_ge(x1_set, sp.snap(b + 2))
                sp.dma_start(x1_dram[b], x1[:].rearrange("p t d -> p (t d)")).then_inc(x1_stored, 16)

            with sp.Fori(0, BATCH - 1) as b:
                batch(b, True)
            batch(BATCH - 1, False)
            sp.wait_ge(x1_stored, 16 * BATCH + 16)

            def ff_batch(b, more):
                if more:
                    sp.wait_ge(y_turned, sp.snap(b + 1))
                    sp.dma_start(y_tok[:].rearrange("p t d -> p (t d)"), x1_dram[b + 1]).then_inc(y_loaded, 16)
                    sp.wait_ge(z2_set[TT - 1], sp.snap(b + 2))
                    sp.dma_start(y_res[:].rearrange("p t d -> p (t d)"), x1_dram[b + 1]).then_inc(y_res_loaded, 16)
                sp.wait_ge(x1_set, sp.snap(b + BATCH + 2))
                sp.dma_start(out[b], x1[:]).then_inc(stored, 16)

            with sp.Fori(0, BATCH - 1) as b:
                ff_batch(b, True)
            ff_batch(BATCH - 1, False)
            sp.wait_ge(stored, 16 * BATCH + 16)

        @block.tensor
        def _(pe):
            pe.wait_ge(m_loaded, 16 * 3)
            for h in range(HEADS):
                mm = pe.matmul(bank[h // 8][:, (h % 8) * 64:(h % 8) * 64 + 64], wqn[:, h], wkn[:, h],
                               start=True, stop=True)
            mm.then_inc(m_made, 1)
            for h in range(HEADS):
                r = 64 if h % 2 == 0 else 0
                mm = pe.matmul(bank[2][r:r + 64, h:h + 1], wkn[:, h], b_qn[:, h:h + 1], start=True, stop=True)
            mm.then_inc(m_made, 1)
            pe.wait_ge(k_loaded, 16 * 4)

            def start():
                pe.wait_ge(g_loaded, 16 * 5)
                pe.wait_ge(wq_full, 1)
                pe.wait_ge(attn_w_set, 1)
                for h in range(HEADS):
                    a = h // 2
                    r = 64 * (h % 2)
                    mm = pe.matmul(bank[a // 2][r:r + 64, (a % 2) * DIM:(a % 2) * DIM + DIM], wv[:, h], wo[:, h],
                                   start=True, stop=True)
                mm.then_inc(g_made, 1)
                pe.wait_ge(consts_set, 5)
                for h in range(HEADS // 2):
                    pe.matmul(u_bank[:, 0:DIM], bv_wide[:, h], wo[:, h], start=(h == 0), stop=False)
                pe.wait_ge(attn_w_set, 2)

            def latent(c, b):
                if c == 0:
                    pe.wait_ge(xt_loaded, pe.snap(16 * b + 16))
                if c == 3:
                    pe.wait_ge(cq_raw_set, pe.snap(b + 1))
                for d in range(DC):
                    mm = pe.matmul(q_bank[c % 3][:], w_a[:, d, c], x_t[:, d], start=(d == 0), stop=(d == DC - 1))
                mm.then_inc(proj[c], 1)

            def between(b):
                pe.wait_ge(q_cos, pe.snap(b * PAIRS + 1))
                for k in range(TT):
                    for d in range(DC):
                        mm = pe.matmul(q_bank[2][:, k * RANK:(k + 1) * RANK], x_t[:, d, k * P:(k + 1) * P],
                                       w_a[:, d, 1, ROPE:P], start=(d == 0), stop=(d == DC - 1))
                mm.then_inc(proj[4], 1)

            def step(T, S, Q, latents=False, values=False):
                def values_of(kt):
                    for h in range(2):
                        slot = BLOCKS.index((h, kt))
                        pe.wait_ge(pt_set[slot], T.n1 if slot < TILES - 2 else T.n2)
                    if kt == 0:
                        pe.wait_ge(v_set, T.b1)
                        pe.wait_ge(u_set, T.n1)
                    for h2 in range(2):
                        mm = pe.matmul(u_bank[64 * h2:64 * h2 + 64, :], v_lat[:, kt], probs_t[:, h2 * TT + kt],
                                       start=(kt == 0), stop=(kt == TT - 1))
                    mm.then_inc(pv[kt], 1)

                for j in range(TILES):
                    h, qt = divmod(j, TT)
                    if T is not None:
                        th, kt = BLOCKS[j]
                        if kt == 0:
                            pe.wait_ge(probs_set[th], T.n1)
                        if j >= 2:
                            pe.wait_ge(pt_set[j - 2], T.n1)
                        else:
                            pe.wait_ge(pt_set[6 + j], T.n1)
                        for q in range(TT):
                            mm = pe.transpose(pt_bank[j % 2][:, q * P:(q + 1) * P],
                                              probs[:, T.buf, th * TT + q, kt * P:(kt + 1) * P], ident[:])
                        mm.then_inc(turned[j], 1)
                    if S is not None:
                        if j == 0:
                            pe.wait_ge(q_hi0_set, S.n1)
                            pe.wait_ge(q_lo0_set, S.n1)
                            pe.wait_ge(k_lo_set, S.b1)
                        if j == TT:
                            pe.wait_ge(q_hi_set, S.n1)
                            pe.wait_ge(q_lo_set, S.n1)
                        pe.wait_ge(exp_done[(j - 2) % TILES], S.n1)
                        cols = slice(qt * P, (qt + 1) * P)
                        pe.matmul(s_bank[j % 2][:], q_hi[:, S.buf, h, cols], k_hi[:, h], start=True, stop=False)
                        pe.matmul(s_bank[j % 2][:], q_hi[:, S.buf, h, cols], k_lo[:, h], start=False, stop=False)
                        pe.matmul(s_bank[j % 2][:], q_lo[:, S.buf, h, cols], k_hi[:, h], start=False,
                                  stop=True).then_inc(scores[j], 1)
                    if latents and j < 4:
                        latent(j, Q.b0)
                    if Q is not None:
                        for c in (Q_AT_BEHIND_LATENTS if latents else Q_AT).get(j, []):
                            if c == 0:
                                pe.wait_ge(staged[Q.buf], pe.snap((Q.b0 * PAIRS + Q.pair) * 8 + (8 if Q.buf else 16)))
                            if c == 0 and latents:
                                pe.wait_ge(cq_set, Q.b1)
                                pe.wait_ge(k_read, pe.snap(3 * Q.b0 + 3))
                            if c == 0 and not latents and not values:
                                for q in range(1, TT):
                                    pe.wait_ge(z_set[q], Q.b1)
                            if c == 2 and values:
                                pe.wait_ge(v_next_set, Q.b1)
                            for s in range(2):
                                mm = pe.matmul(q_bank[c][:], wq_stage[:, Q.buf, s, c * P:(c + 1) * P], cq[:],
                                               start=(s == 0), stop=(s == 1))
                            mm.then_inc(qproj[c], 1)
                    if T is not None and j in VALUES_AT:
                        values_of(VALUES_AT[j])
                    if T is None and values:
                        bh = HEADS // 2 + j
                        mm = pe.matmul(u_bank[:, 0:DIM], bv_wide[:, bh], wo[:, bh], start=False,
                                       stop=(bh == HEADS - 1))
                        if j == TILES - 1:
                            mm.then_inc(g_made, 1)
                if T is not None:
                    values_of(VALUES_AT[TILES])
                elif values:
                    pe.wait_ge(attn_w_set, 3)

            def turn(b, later):
                pe.wait_ge(y_loaded, pe.snap(16 * b + 16))
                if later:
                    for m in range(2):
                        pe.wait_ge(half_set[m], pe.snap(b * (UNITS // 2)))
                for d in range(DC):
                    for q in range(TT):
                        mm = pe.transpose(bank[d][:, q * P:(q + 1) * P], y_tok[:, q, d * P:(d + 1) * P], ident[:])
                mm.then_inc(y_turned, 1)

            def route(b, later):
                pe.wait_ge(y_raw_set, pe.snap(b + 1))
                if later:
                    pe.wait_ge(gated[0], pe.snap(b * (ROUTED // 2)))
                for q in range(TT):
                    for d in range(DC):
                        mm = pe.matmul(bank[2][:, q * EXPERTS:(q + 1) * EXPERTS], y_raw[:, d, q * P:(q + 1) * P],
                                       w_g[:, d], start=(d == 0), stop=(d == DC - 1))
                mm.then_inc(routed, 1)

            def finish(b, more):
                def project(q, pairs):
                    cols = slice(q * P, (q + 1) * P)
                    for a in pairs:
                        dst = q_bank[q % 3][:, 0:DIM]
                        pe.matmul(dst, u_hi[:, a, cols], g_hi[:, a], start=(a == 0), stop=False)
                        pe.matmul(dst, u_hi[:, a, cols], g_lo[:, a], start=False, stop=False)
                        mm = pe.matmul(dst, u_lo[:, a, cols], g_hi[:, a], start=False, stop=(a == PAIRS - 1))
                    if a == PAIRS - 1:
                        mm.then_inc(oproj[q], 1)
                pe.wait_ge(u_set, pe.snap(b * PAIRS + PAIRS))
                if more:
                    pe.wait_ge(q_cos, pe.snap(b * PAIRS + PAIRS + 2))
                for q in range(3):
                    project(q, range(PAIRS - 1))
                if not more:
                    turn(0, False)
                pe.wait_ge(u_set, pe.snap(b * PAIRS + PAIRS + 1))
                for q in range(3):
                    project(q, [PAIRS - 1])
                pe.wait_ge(z_set[0], pe.snap(b + 2))
                project(3, range(PAIRS))
                if not more:
                    pe.wait_ge(small_loaded, 16 * 6)
                    route(0, False)

            walk(pe, step, between, finish, start)

            def product(dst, w, unit):
                for d in range(DC):
                    pe.matmul(dst, w[:, 0, d, unit], y_hi[:, d], start=(d == 0), stop=False)
                    pe.matmul(dst, w[:, 1, d, unit], y_hi[:, d], start=False, stop=False)
                    mm = pe.matmul(dst, w[:, 0, d, unit], y_lo[:, d], start=False, stop=(d == DC - 1))
                return mm

            def ff_batch(b, more):
                b1 = pe.snap(b + 1)
                b2 = pe.snap(b + 2)
                at = [pe.snap(b * (UNITS // 2) + k) for k in range(UNITS // 2 + 2)]
                at_e = [pe.snap(b * (ROUTED // 2) + k) for k in range(ROUTED // 2 + 1)]
                pe.wait_ge(y_hi_set, b1)
                pe.wait_ge(y_lo_set, b1)
                for u in range(UNITS):
                    if u >= 2:
                        pe.wait_ge(half_set[u % 2], at[u // 2])
                    if u >= SHARED + 2:
                        pe.wait_ge(gated[u % 2], at_e[u // 2 - 1])
                    if u < SHARED:
                        product(bank[u % 2][:], w_sh_v, u).then_inc(pre[u % 2], 1)
                    else:
                        product(bank[u % 2][:], w_in_v, u - SHARED)
                        if u == SHARED:
                            pe.wait_ge(route_step, pe.snap(ROUTE_STEPS * b + 1))
                        product(bank[2 + u % 2][:], w_in_v, ROUTED + u - SHARED).then_inc(pre[u % 2], 1)
                    if u == 1:
                        pe.wait_ge(route_step, pe.snap(ROUTE_STEPS * b + ROUTE_STEPS))
                        pe.wait_ge(z2_set[3], b1)
                        for q in range(TT):
                            mm = pe.transpose(bank[7][0:EXPERTS, q * P:(q + 1) * P], w_tok[:, q], ident[:])
                        mm.then_inc(w_turned, 1)
                    if u >= SHARED:
                        if u == SHARED + 1:
                            pe.wait_ge(fw_hi_set, 3)
                            pe.wait_ge(w_hi_set, b1)
                            pe.wait_ge(w_lo_set, b1)
                        if u >= SHARED + 2:
                            pe.wait_ge(h_set[u % 2], at[u // 2])
                        for e in {SHARED: [], SHARED + 1: [0, 1]}.get(u, [u - SHARED]):
                            for s in range(2):
                                mm = pe.matmul(bank[4 + e % 2][:], sel[:, e], w_t_split[:, s],
                                               start=(s == 0), stop=(s == 1))
                            mm.then_inc(widened[e % 2], 1)
                if more:
                    nb = pe.snap(b + 1)
                    turn(nb, True)
                pe.wait_ge(fw_hi_set, 4)
                pe.wait_ge(out_lo_set, 1)

                def project(q, units):
                    dst = bank[6 + q % 2][:, 0:DIM]
                    cols = slice(q * P, (q + 1) * P)
                    for u in units:
                        if u == 0:
                            pe.wait_ge(z2_set[(q - 2) % TT], b2 if q >= 2 else b1)
                            pe.matmul(dst, w_t[:, cols], b_down[:], start=True, stop=False)
                        if q == 0:
                            pe.wait_ge(h_hi_set[u % 2], at[u // 2 + 1])
                            pe.wait_ge(h_lo_set[u % 2], at[u // 2 + 2])
                        pe.matmul(dst, h_hi[:, u, cols], w_out_hi[:, u], start=False, stop=False)
                        pe.matmul(dst, h_hi[:, u, cols], w_out_lo[:, u], start=False, stop=False)
                        mm = pe.matmul(dst, h_lo[:, u, cols], w_out_hi[:, u], start=False, stop=(u == UNITS - 1))
                    if u == UNITS - 1:
                        mm.then_inc(down[q], 1)
                for q in range(2):
                    project(q, range(UNITS - 1))
                for q in range(2):
                    project(q, [UNITS - 1])
                if more:
                    route(nb, True)
                for q in range(2, TT):
                    project(q, range(UNITS))

            pe.wait_ge(fw_hi_set, 2)
            pe.wait_ge(fw_lo_set, 2)
            for i in range(TT):
                pe.wait_ge(z_set[i], BATCH + 1)
            with pe.Fori(0, BATCH - 1) as b:
                ff_batch(b, True)
            ff_batch(BATCH - 1, False)

        @block.scalar
        def _(act):
            act.wait_ge(m_made, 1)
            act.wait_ge(q_loaded, 16 * 2)
            for k in range(2):
                m4 = bank[k][:].rearrange("p (a s j) -> p a s j", s=2, j=64)
                act.copy(wq_raw[:, 4 * k:4 * k + 4, 0, 64:128], m4[:, :, 0, :])
                last = act.copy(wq_raw[:, 4 * k:4 * k + 4, 1, 0:64], m4[:, :, 1, :])
            last.then_inc(wq_full, 1)
            act.wait_ge(wq_full, 1)
            act.copy(wq_split[:, :, 0, :], wq_raw.rearrange("p a c m -> p a (c m)")).then_inc(wq_hi_set, 1)
            act.wait_ge(k_loaded, 16 * 4)

            def start():
                act.wait_ge(g_made, 1)
                for k in range(4):
                    act.copy(g_hi[:, 2 * k:2 * k + 2, :], bank[k][:].rearrange("p (a n) -> p a n", a=2))\
                       .then_inc(g_hi_set, 1)

            def step(T, S, Q, latents=False, values=False):
                def exp(j):
                    act.wait_ge(rowmax[j], S.n1)
                    act.activation(probs[:, S.buf, j], s_bank[j % 2][:], ACT.Exp,
                                   bias=neg_max[:, S.buf, j:j + 1],
                                   accum_out=sums[:, S.buf, j:j + 1]).then_inc(exp_done[j], 1)

                def exp_last(j):
                    if S is not None and j >= 1:
                        exp(j - 1)

                def copy_block(j):
                    if T is not None:
                        act.wait_ge(turned[j], T.n1)
                        h, kt = BLOCKS[j]
                        act.wait_ge(pv[kt], T.n1)
                        act.copy(probs_t[:, h * TT + kt], pt_bank[j % 2][:]).then_inc(pt_set[j], 1)

                def q_high(c):
                    act.wait_ge(q_added if c else q_added0, Q.n1)
                    act.copy(q_hi[:, Q.buf, c], roped[:, c]).then_inc(q_hi_set if c else q_hi0_set, 1)
                for j in range(TILES):
                    if j == 5:
                        exp_last(j)
                        copy_block(j)
                    else:
                        copy_block(j)
                        exp_last(j)
                    if latents and j == 1:
                        act.wait_ge(proj[0], Q.b1)
                        act.activation(cq_raw[:], q_bank[0][:], ACT.Identity, bias=b_a[:, 0:1])\
                            .then_inc(cq_raw_set, 1)
                        act.wait_ge(cq_raw_set, Q.b1)
                        act.copy(cq[:], cq_raw[:]).then_inc(cq_hi_set, 1)
                    if Q is not None and not latents and j == 5:
                        q_high(0)
                    if Q is not None and not latents and j == 7:
                        q_high(1)
                if latents:
                    act.wait_ge(k_full, act.snap(2 * Q.b0 + 2))
                    if S is not None:
                        act.wait_ge(scores[TILES - 1], S.n1)
                    act.activation(k_hi[:], k_rope[:], ACT.Identity, scale=SCALE).then_inc(k_hi_set, 1)
                if S is not None:
                    exp(TILES - 1)
                if latents:
                    q_high(0)
                    q_high(1)
                if T is not None:
                    act.wait_ge(pv[TT - 1], T.n2)
                    act.copy(u_hi[:, T.pair], u_bank[:]).then_inc(u_hi_set, 1)
                if values:
                    act.wait_ge(v_next_set, Q.b1)
                    act.copy(v_lat[:], v_next[:]).then_inc(v_set, 1)

            walk(act, step, lambda b: None, lambda b, more: None, start)

            def take_rows(b):
                act.wait_ge(y_turned, act.snap(b + 1))
                act.copy(y_raw[:, 0], bank[0][:])
                act.copy(y_raw[:, 1], bank[1][:]).then_inc(y_raw_set, 1)
                act.wait_ge(y_raw_set, act.snap(b + 1))
                act.copy(y_hi[:], y_raw[:]).then_inc(y_hi_set, 1)
                act.wait_ge(route_step, act.snap(ROUTE_STEPS * b + ROUTE_EXP))
                act.activation(odds[:], shifted[:], ACT.Exp).then_inc(odds_set, 1)

            def ff_batch(b, more):
                b1 = act.snap(b + 1)
                at = [act.snap(b * (UNITS // 2) + k) for k in range(UNITS // 2 + 2)]
                at_e = [act.snap(b * (ROUTED // 2) + k) for k in range(ROUTED // 2 + 1)]

                def split_hi(u):
                    act.wait_ge(h_set[u % 2], at[u // 2 + 1])
                    act.copy(h_hi[:, u], hidden[:, u % 2]).then_inc(h_hi_set[u % 2], 1)

                for u in range(UNITS):
                    act.wait_ge(pre[u % 2], at[u // 2 + 1])
                    if u >= SHARED + 2:
                        act.wait_ge(silu_set[u % 2], at_e[u // 2 - 1])
                    act.activation(half_pre[:, u % 2], bank[u % 2][:], ACT.Identity, bias=b_pre[:, u:u + 1],
                                   scale=0.5).then_inc(half_set[u % 2], 1)
                    act.wait_ge(half_set[u % 2], at[u // 2 + 1])
                    act.activation(tanh_pre[:, u % 2], half_pre[:, u % 2], ACT.Tanh).then_inc(tanh_set[u % 2], 1)
                    if u == 1:
                        act.wait_ge(w_turned, b1)
                        act.copy(w_t, bank[7][0:EXPERTS, :]).then_inc(w_t_set, 1)
                        act.wait_ge(w_t_set, b1)
                        act.copy(w_t_split[:, 0], w_t).then_inc(w_hi_set, 1)
                    if u >= 1:
                        split_hi(u - 1)
                split_hi(UNITS - 1)
                if more:
                    take_rows(act.snap(b + 1))

            act.wait_ge(fw_loaded, 16 * 2)
            act.copy(wq_stage[:].rearrange(flat)[:, 0:n_sh], raw_sh).then_inc(fw_hi_set, 1)
            act.copy(wq_split[:].rearrange(flat)[:, 0:n_in], raw_in).then_inc(fw_hi_set, 1)
            take_rows(0)
            act.wait_ge(fw_late_loaded, 16 * 2)
            act.copy(sel, sel_raw).then_inc(fw_hi_set, 1)
            act.wait_ge(oproj[TT - 1], BATCH)
            act.copy(w_out_hi[:], raw_out).then_inc(fw_hi_set, 1)
            act.wait_ge(consts_set, 6)
            with act.Fori(0, BATCH - 1) as b:
                ff_batch(b, True)
            ff_batch(BATCH - 1, False)

        @block.vector
        def _(dve):
            dve.memset(ones[:], 1.0).then_inc(consts_set, 1)
            dve.memset(minus_half[:], -0.5).then_inc(consts_set, 1)
            dve.memset(w_tok[:], 0.0).then_inc(consts_set, 1)
            dve.wait_ge(consts_set, 3)
            dve.memset(w_tok[:, :, ROUTED:ROUTED + 1], 1.0).then_inc(consts_set, 1)
            dve.wait_ge(q_loaded, 16 * 2)
            dve.wait_ge(m_made, 2)
            bm = bank[2][:, 0:HEADS].rearrange("p (a s) -> p a s", s=2)
            dve.tensor_copy(b_q[64:128, :, 0], bm[64:128, :, 0])
            dve.tensor_copy(b_q[0:64, :, 1], bm[0:64, :, 1]).then_inc(attn_w_set, 1)
            dve.wait_ge(wq_hi_set, 1)
            dve.tensor_tensor(wq_split[:, :, 1, :], wq_raw.rearrange("p a c m -> p a (c m)"),
                              wq_split[:, :, 0, :].bitcast(F32), ALU.subtract).then_inc(wq_lo_set, 1)
            dve.wait_ge(k_loaded, 16 * 4)

            def start():
                dve.wait_ge(g_loaded, 16 * 5)
                for h in range(HEADS):
                    last = dve.tensor_scalar(bv_wide[:, h], ones[:], b_v[:, h:h + 1], None, ALU.mult)
                last.then_inc(consts_set, 1)
                for k in range(4):
                    dve.wait_ge(g_hi_set, k + 1)
                    last = dve.tensor_tensor(g_lo[:, 2 * k:2 * k + 2, :], bank[k][:].rearrange("p (a n) -> p a n", a=2),
                                             g_hi[:, 2 * k:2 * k + 2, :].bitcast(F32), ALU.subtract)
                last.then_inc(attn_w_set, 1)
                dve.wait_ge(small_loaded, 16 * 6)
                dve.tensor_scalar(b_pre[:], b_pre[:], 0.5, None, ALU.mult).then_inc(consts_set, 1)

            def row_stats(n, q, z_done, b2):
                dve.wait_ge(z_done[q], b2)
                if q >= 1:
                    dve.wait_ge(stats_set, dve.snap(TT * n + q))
                dve.bn_stats(stats[:, q], z[:, q]).then_inc(stats_set, 1)
                if q >= 1:
                    op = dve.bn_aggr(mv[:, q - 1], stats[:, q - 1])
                    if q == TT - 1:
                        op.then_inc(mv_set, 1)

            def last_stats(n):
                dve.wait_ge(stats_set, dve.snap(TT * n + TT))
                dve.wait_ge(mv_set, dve.snap(2 * n + 1))
                dve.tensor_scalar(var_e[:, 0:TT - 1], mv[:, 0:TT - 1, 1], EPS, None, ALU.add)
                dve.bn_aggr(mv[:, TT - 1], stats[:, TT - 1]).then_inc(mv_set, 1)
                dve.wait_ge(mv_set, dve.snap(2 * n + 2))
                dve.tensor_scalar(var_e[:, TT - 1:], mv[:, TT - 1:, 1], EPS, None, ALU.add)\
                   .then_inc(var_set, 1)

            def step(T, S, Q, latents=False, values=False):
                def normalise(j):
                    dve.wait_ge(exp_done[j], S.n1 if j < 6 else S.n2)
                    dve.reciprocal(inv[:, S.buf, j:j + 1], sums[:, S.buf, j:j + 1]).then_inc(inv_set[j], 1)
                    dve.wait_ge(inv_set[j], S.n1)
                    op = dve.tensor_scalar(probs[:, S.buf, j], probs[:, S.buf, j], inv[:, S.buf, j:j + 1],
                                           None, ALU.mult)
                    if j % TT == TT - 1:
                        op.then_inc(probs_set[j // TT], 1)

                def key(c):
                    dve.wait_ge(proj[c + 1], Q.b1)
                    dve.scalar_tensor_tensor(out=k_rope[:, c] if c < 2 else rot[:], in0=q_bank[(c + 1) % 3][:],
                                             scalar=b_a[:, c + 1:c + 2], in1=rope[:, c],
                                             op0=ALU.add, op1=ALU.mult).then_inc(k_read, 1)

                def query(c):
                    dve.wait_ge(qproj[c], Q.n1 if c < 2 else dve.snap(Q.b0 * PAIRS + Q.pair + 3))
                    if c == 1 and S is not None:
                        dve.wait_ge(q_lo_set, S.n1)
                    op = dve.scalar_tensor_tensor(out=roped[:, c] if c < 2 else rot[:], in0=q_bank[c][:],
                                                  scalar=b_q[:, Q.pair, c:c + 1], in1=rope[:, c],
                                                  op0=ALU.add, op1=ALU.mult)
                    if c == 2:
                        op.then_inc(q_cos, 1)
                for j in range(TILES):
                    if S is not None:
                        dve.wait_ge(scores[j], S.n1)
                        dve.tensor_reduce(neg_max[:, S.buf, j:j + 1], s_bank[j % 2][:], AX.X, ALU.max,
                                          negate=True).then_inc(rowmax[j], 1)
                    if latents:
                        if 1 <= j <= 3:
                            key(j - 1)
                        if j == 2:
                            dve.wait_ge(cq_hi_set, Q.b1)
                            dve.tensor_tensor(cq[64:128], cq_raw[64:128], cq[64:128].bitcast(F32), ALU.subtract)\
                               .then_inc(cq_set, 1)
                        if j == 4:
                            dve.wait_ge(k_read, dve.snap(3 * Q.b0 + 3))
                            dve.tensor_tensor(k_rope[0:64, 0], k_rope[0:64, 0], rot[0:64], ALU.add)\
                               .then_inc(k_full, 1)
                            dve.tensor_tensor(k_rope[64:128, 1], k_rope[64:128, 1], rot[64:128], ALU.add)\
                               .then_inc(k_full, 1)
                        if j == 5:
                            query(0)
                            query(1)
                        if j == 6:
                            dve.wait_ge(k_full, dve.snap(2 * Q.b0 + 2))
                            query(2)
                    elif Q is not None and 1 <= j <= 3:
                        query(j - 1)
                    if S is not None and j >= 1:
                        normalise(j - 1)
                if latents:
                    dve.wait_ge(k_hi_set, Q.b1)
                    dve.scalar_tensor_tensor(out=k_lo[:], in0=k_rope[:], scalar=SCALE, in1=k_hi[:].bitcast(F32),
                                             op0=ALU.mult, op1=ALU.subtract).then_inc(k_lo_set, 1)
                if T is None and values:
                    dve.wait_ge(g_made, 2)
                    dve.tensor_tensor(b_o[:], u_bank[:, 0:DIM], b_o[:], ALU.add).then_inc(attn_w_set, 1)
                if S is not None:
                    normalise(TILES - 1)
                if latents:
                    dve.wait_ge(proj[4], Q.b1)
                    dve.tensor_tensor(v_next[:], q_bank[2][:, 0:TT * RANK].rearrange("p (k r) -> p k r", k=TT),
                                      b_kv[:].rearrange("p (a r) -> p a r", a=1).to_broadcast([P, TT, RANK]),
                                      ALU.add).then_inc(v_next_set, 1)
                if T is not None:
                    dve.wait_ge(u_hi_set, T.n1)
                    dve.tensor_tensor(u_lo[:, T.pair], u_bank[:], u_hi[:, T.pair].bitcast(F32), ALU.subtract)\
                       .then_inc(u_set, 1)

            def low_rows(b):
                dve.wait_ge(y_hi_set, dve.snap(b + 1))
                dve.tensor_tensor(y_lo[:], y_raw[:], y_hi[:].bitcast(F32), ALU.subtract).then_inc(y_lo_set, 1)

            def route(b):
                steps = [0]

                def then(ins):
                    steps[0] += 1
                    ins.then_inc(route_step, 1)
                    dve.wait_ge(route_step, dve.snap(ROUTE_STEPS * b + steps[0]))
                dve.wait_ge(routed, dve.snap(b + 1))
                e3 = [P, TT, EXPERTS]
                then(dve.tensor_tensor(gate[:], bank[2][:, 0:TT * EXPERTS].rearrange("p (t e) -> p t e", t=TT),
                                       b_g[:].rearrange("p (a e) -> p a e", a=1).to_broadcast(e3), ALU.add))
                then(dve.tensor_reduce(top[:], gate[:], AX.X, ALU.max, negate=True))
                then(dve.tensor_tensor(shifted[:], gate[:],
                                       top[:].rearrange("p (t a) -> p t a", a=1).to_broadcast(e3), ALU.add))
                assert steps[0] == ROUTE_EXP
                other = gate[:].rearrange("p t (a f) -> p t a f", a=1).to_broadcast([P, TT, EXPERTS, EXPERTS])
                own = gate[:].rearrange("p t (e a) -> p t e a", a=1).to_broadcast([P, TT, EXPERTS, EXPERTS])
                then(dve.tensor_tensor(above, other, own, ALU.is_gt))
                then(dve.tensor_tensor(ties, other, own, ALU.is_equal))
                f3 = "p t e f -> p t (e f)"
                then(dve.tensor_tensor(ties.rearrange(f3), ties.rearrange(f3),
                                       before[:].rearrange("p (a e) -> p a e", a=1).to_broadcast([P, TT, 64]),
                                       ALU.mult))
                then(dve.tensor_tensor(above, above, ties, ALU.add))
                then(dve.tensor_reduce(rank[:], above, AX.X, ALU.add))
                then(dve.tensor_scalar(chosen[:], rank[:], float(ROUTED), None, ALU.is_lt))
                dve.wait_ge(odds_set, dve.snap(b + 1))
                then(dve.tensor_tensor(picked[:], odds[:], chosen[:], ALU.mult))
                then(dve.tensor_reduce(total[:], picked[:], AX.X, ALU.add))
                then(dve.reciprocal(inv_total[:], total[:]))
                then(dve.tensor_tensor(w_tok[:, :, 0:ROUTED], picked[:, :, 0:ROUTED],
                                       inv_total[:].rearrange("p (t a) -> p t a", a=1).to_broadcast([P, TT, ROUTED]),
                                       ALU.mult))
                assert steps[0] == ROUTE_STEPS

            def split_low():
                for n, (lo, raw, hi) in enumerate((
                        (wq_stage[:].rearrange(flat)[:, n_sh:2 * n_sh], raw_sh, wq_stage[:].rearrange(flat)[:, 0:n_sh]),
                        (wq_split[:].rearrange(flat)[:, n_in:2 * n_in], raw_in, wq_split[:].rearrange(flat)[:, 0:n_in]))):
                    dve.wait_ge(fw_hi_set, n + 1)
                    dve.tensor_tensor(lo, raw, hi.bitcast(F32), ALU.subtract).then_inc(fw_lo_set, 1)

            def finish(b, more):
                b1 = dve.snap(b + 1)
                if not more:
                    split_low()
                    low_rows(0)
                b2 = dve.snap(b + 2)
                dve.wait_ge(xb_set, b1)
                dve.wait_ge(x1_set, b1)

                def add(q):
                    dve.wait_ge(oproj[q], b1)
                    dve.tensor_tensor(z[:, q], q_bank[q % 3][:, 0:DIM], x_b[:, q], ALU.add).then_inc(z_set[q], 1)
                for q in range(TT - 1):
                    add(q)
                for q in range(TT - 1):
                    row_stats(b, q, z_set, b2)
                add(TT - 1)
                row_stats(b, TT - 1, z_set, b2)
                last_stats(b)
                if not more:
                    route(0)

            walk(dve, step, lambda b: None, finish, start)

            def ff_batch(b, more):
                b1 = dve.snap(b + 1)
                b2 = dve.snap(b + 2)
                at = [dve.snap(b * (UNITS // 2) + k) for k in range(UNITS // 2 + 2)]
                at_e = [dve.snap(b * (ROUTED // 2) + k) for k in range(ROUTED // 2 + 1)]
                for u in range(UNITS):
                    if u == SHARED:
                        dve.wait_ge(w_hi_set, b1)
                        dve.tensor_tensor(w_t_split[:, 1], w_t, w_t_split[:, 0].bitcast(F32), ALU.subtract)\
                           .then_inc(w_lo_set, 1)
                    dve.wait_ge(tanh_set[u % 2], at[u // 2 + 1])
                    if u >= 2:
                        dve.wait_ge(h_hi_set[u % 2], at[u // 2])
                    dve.wait_ge(h_lo_set[u % 2], at[u // 2 + 1])
                    op = dve.scalar_tensor_tensor(out=hidden[:, u % 2], in0=tanh_pre[:, u % 2], scalar=1.0,
                                                  in1=half_pre[:, u % 2], op0=ALU.add, op1=ALU.mult)
                    if u < SHARED:
                        op.then_inc(h_set[u % 2], 1)
                        continue
                    op.then_inc(silu_set[u % 2], 1)
                    dve.wait_ge(silu_set[u % 2], at_e[u // 2])
                    dve.scalar_tensor_tensor(out=hidden[:, u % 2], in0=bank[2 + u % 2][:], scalar=b_up[:, u:u + 1],
                                             in1=hidden[:, u % 2], op0=ALU.add, op1=ALU.mult).then_inc(gated[u % 2], 1)
                    dve.wait_ge(gated[u % 2], at_e[u // 2])
                    dve.wait_ge(widened[u % 2], at_e[u // 2])
                    dve.tensor_tensor(hidden[:, u % 2], bank[4 + u % 2][:], hidden[:, u % 2], ALU.mult)\
                       .then_inc(h_set[u % 2], 1)
                if more:
                    nb = dve.snap(b + 1)
                    low_rows(nb)
                dve.wait_ge(y_res_loaded, dve.snap(16 * b + 16))
                dve.wait_ge(x1_set, dve.snap(b + BATCH + 1))

                def add(q):
                    dve.wait_ge(down[q], b1)
                    dve.tensor_tensor(z[:, q], bank[6 + q % 2][:, 0:DIM], y_res[:, q], ALU.add).then_inc(z2_set[q], 1)
                add(0)
                add(1)
                if more:
                    route(nb)
                row_stats(b + BATCH, 0, z2_set, b2)
                row_stats(b + BATCH, 1, z2_set, b2)
                for q in (2, 3):
                    add(q)
                    row_stats(b + BATCH, q, z2_set, b2)
                last_stats(b + BATCH)

            with dve.Fori(0, BATCH - 1) as b:
                ff_batch(b, True)
            ff_batch(BATCH - 1, False)

        @block.gpsimd
        def _(pool):
            for s, n in [(done, 1) for done in z_set] + [(qproj[2], 2)] + [(s, 1) for s in exp_done[6:] + pt_set[6:] + pv]\
                    + [(u_set, 1), (x1_set, 1)] + [(s, 1) for s in z2_set + h_lo_set] + [(stored, 16), (x1_stored, 16)]:
                pool.sem_inc(s, n)
            pool.wait_ge(consts_set, 2)
            def normalise_rows(n, stored_rows, value):
                wide = [P, TT, DIM]
                pool.wait_ge(var_set, pool.snap(n + 1))
                pool.tensor_tensor(rstd[:], var_e[:], minus_half[:], ALU.pow).then_inc(rstd_set, 1)
                pool.wait_ge(stored_rows, value)
                pool.tensor_tensor(x1[:], z[:], mv[:, :, 0:1].to_broadcast(wide), ALU.subtract)\
                    .then_inc(rstd_set, 1)
                pool.wait_ge(rstd_set, pool.snap(2 * n + 2))
                pool.tensor_tensor(x1[:], x1[:], rstd[:].rearrange("p (t a) -> p t a", a=1).to_broadcast(wide),
                                   ALU.mult).then_inc(x1_set, 1)

            def step(T, S, Q, latents=False, values=False):
                if Q is None:
                    return

                def add(c):
                    rows = slice(64 * c, 64 * c + 64)
                    pool.tensor_tensor(roped[rows, c], roped[rows, c], rot[rows], ALU.add)\
                        .then_inc(q_added if c else q_added0, 1)

                def low(c):
                    pool.wait_ge(q_hi_set if c else q_hi0_set, Q.n1)
                    pool.tensor_tensor(q_lo[:, Q.buf, c], roped[:, c], q_hi[:, Q.buf, c].bitcast(F32), ALU.subtract)\
                        .then_inc(q_lo_set if c else q_lo0_set, 1)
                pool.wait_ge(q_cos, Q.n1)
                add(0)
                pool.wait_ge(q_added0, Q.n1)
                add(1)
                pool.wait_ge(q_added, Q.n1)
                low(0)
                low(1)

            def finish(b, more):
                pool.wait_ge(attn_w_set, 3)
                pool.wait_ge(x_loaded, pool.snap(16 * b + 16))
                for i in range(TT):
                    last = pool.tensor_tensor(x_b[:, i], x_tok[:, i], b_o[:], ALU.add)
                last.then_inc(xb_set, 1)
                normalise_rows(b, x1_stored, pool.snap(16 * b + 16))

            walk(pool, step, lambda b: None, finish)

            pool.wait_ge(fw_hi_set, 4)
            pool.tensor_tensor(w_out_lo[:], raw_out, w_out_hi[:].bitcast(F32), ALU.subtract).then_inc(out_lo_set, 1)
            with pool.Fori(0, BATCH) as b:
                b1 = pool.snap(b + 1)
                at = [pool.snap(b * (UNITS // 2) + k) for k in range(UNITS // 2 + 2)]
                for u in range(UNITS):
                    pool.wait_ge(h_hi_set[u % 2], at[u // 2 + 1])
                    pool.tensor_tensor(h_lo[:, u], hidden[:, u % 2], h_hi[:, u].bitcast(F32), ALU.subtract)\
                        .then_inc(h_lo_set[u % 2], 1)
                normalise_rows(b + BATCH, stored, pool.snap(16 * b + 16))


def layouts(inputs):
    g = {k.replace("L0_", ""): np.asarray(v) for k, v in inputs.items()}
    even, odd = np.arange(0, ROPE, 2), np.arange(1, ROPE, 2)
    pe, rt = np.concatenate([even, odd]), np.concatenate([odd, even])
    cat = np.concatenate
    x = g["attn_x"]
    o = {}
    o["x"] = x.reshape(BATCH, TT, P, DIM).transpose(0, 2, 1, 3)
    o["xT"] = x.reshape(BATCH * SEQ, DC, P).transpose(2, 1, 0)
    wqa, wkva = g["attn_wq_a_w"], g["attn_wkv_a_w"]
    kv, kpe, krt = wkva[:, :RANK], wkva[:, RANK + pe], wkva[:, RANK + rt]
    w_a = np.stack([cat([wqa, wqa], 1), cat([kpe, kv], 1), cat([kv, kpe], 1), cat([krt, krt], 1)], 1)
    o["w_a"] = w_a.reshape(DC, P, 4, P).transpose(1, 0, 2, 3)
    bqa, bkva = g["attn_wq_a_b"], g["attn_wkv_a_b"]
    bkv, bpe, brt = bkva[:RANK], bkva[RANK + pe], bkva[RANK + rt]
    o["b_a"] = np.stack([cat([bqa, bqa]), cat([bpe, bkv]), cat([bkv, bpe]), cat([brt, brt])], 1)
    o["b_kv"] = bkv[None]
    wqb = g["attn_wq_b_w"].reshape(RANK, HEADS, NOPE + ROPE)
    bqb = g["attn_wq_b_b"].reshape(HEADS, NOPE + ROPE)
    wkvb = g["attn_wkv_b_w"].reshape(RANK, HEADS, NOPE + VHD)
    bkvb = g["attn_wkv_b_b"].reshape(HEADS, NOPE + VHD)
    qn = wqb[:, :, :NOPE].transpose(2, 1, 0)
    o["wqn"] = cat([qn, qn], 2)
    o["wkn"] = wkvb[:, :, :NOPE].transpose(2, 1, 0)
    o["wv"] = wkvb[:, :, NOPE:].transpose(2, 1, 0)
    o["wo"] = g["attn_wo_w"].reshape(HEADS, VHD, DIM).transpose(1, 0, 2)
    o["b_qn"] = bqb[:, :NOPE].T
    o["b_v"] = bkvb[:, NOPE:].T
    o["b_o"] = g["attn_wo_b"][None]
    raw = np.zeros((P, PAIRS, 3, P), np.float32)
    b_q = np.zeros((P, PAIRS, 4), np.float32)
    for r in (slice(0, 64), slice(64, 128)):
        raw[r, :, 0, 0:64] = wqb[:, 0::2, NOPE + pe]
        raw[r, :, 1, 64:128] = wqb[:, 1::2, NOPE + pe]
        raw[r, :, 2, 0:64] = wqb[:, 0::2, NOPE + rt]
        raw[r, :, 2, 64:128] = wqb[:, 1::2, NOPE + rt]
    b_q[0:64, :, 0] = bqb[0::2, NOPE + pe].T
    b_q[64:128, :, 1] = bqb[1::2, NOPE + pe].T
    b_q[0:64, :, 2] = bqb[0::2, NOPE + rt].T
    b_q[64:128, :, 2] = bqb[1::2, NOPE + rt].T
    o["wq_raw"], o["b_q"] = raw, b_q
    def cols(w):
        return w.reshape(-1, DC, P, HID).transpose(2, 1, 0, 3)
    ws = g["ffn_Ws_up"].reshape(DIM, SHARED, HID).transpose(1, 0, 2)
    o["w_in"] = cols(cat([g["ffn_Wgate"], g["ffn_Wup"]], 0)).reshape(P, -1)
    o["w_sh"] = cols(ws).reshape(P, -1)
    o["w_out"] = cat([g["ffn_Ws_down"].reshape(SHARED, HID, DIM), g["ffn_Wdown"]], 0).transpose(1, 0, 2)
    o["w_g"] = g["ffn_Wg"].reshape(DC, P, EXPERTS).transpose(1, 0, 2)
    o["b_g"] = g["ffn_bg"][None]
    o["b_pre"] = cat([g["ffn_bs_up"].reshape(SHARED, HID), g["ffn_bgate"]], 0).T
    o["b_up"] = cat([np.zeros((SHARED, HID), np.float32), g["ffn_bup"]], 0).T
    o["b_down"] = cat([g["ffn_bdown"], g["ffn_bs_down"][None], np.zeros((1, DIM), np.float32)], 0)
    sel = np.zeros((EXPERTS, ROUTED, P), np.float32)
    for u in range(ROUTED):
        sel[u, u] = 1
    o["sel"] = sel
    o["before"] = np.tril(np.ones((EXPERTS, EXPERTS), np.float32), -1).reshape(1, -1)
    f = np.float32
    inv_freq = (f(1.0) / np.power(f(THETA), np.arange(0, ROPE, 2, dtype=f) / f(ROPE))).astype(f)
    ang = np.outer(np.arange(SEQ, dtype=f), inv_freq).astype(f)
    c, s = np.cos(ang).T.astype(f), np.sin(ang).T.astype(f)
    cc, ss, one = cat([c, c]), cat([-s, s]), np.ones((64, SEQ), f)
    o["rope"] = np.stack([cat([cc, one]), cat([one, cc]), cat([ss, ss])], 1)
    o["ident"] = np.eye(P, dtype=f)
    return {k: np.ascontiguousarray(v) for k, v in o.items()}


def kernel(**inputs):
    import concourse.bacc as bacc
    from concourse.bass_utils import run_bass_kernel_spmd

    nc = bacc.Bacc("TRN2", target_bir_lowering=False, num_devices=1)
    arrays, t = {}, {}
    for name, a in layouts(inputs).items():
        arrays[f"in_{name}"] = a
        t[name] = nc.dram_tensor(f"in_{name}", a.shape, mybir.dt.from_np(a.dtype), kind="ExternalInput").ap()
    out = nc.dram_tensor("out", (BATCH, SEQ, DIM), F32, kind="ExternalOutput").ap()
    program(nc, t, out.rearrange("b (t p) d -> b p t d", p=P))
    r = run_bass_kernel_spmd(nc, [arrays], core_ids=[0])
    return np.asarray(r.results[0]["out"])
```
